# Optimizing a Trainium2 kernel written in Bass

```python
import numpy as np
import jax
import jax.numpy as jnp

def _softmax(x, axis=-1):
    return jax.nn.softmax(x, axis=axis)

def _gelu(x):
    return jax.nn.gelu(x, approximate=True)

def _silu(x):
    return jax.nn.silu(x)

def _sigmoid(x):
    return jax.nn.sigmoid(x)

def _layernorm(x, axis=-1, eps=1e-05):
    m = jnp.mean(x, axis=axis, keepdims=True)
    v = jnp.var(x, axis=axis, keepdims=True)
    return (x - m) / jnp.sqrt(v + eps)

def _scatter_add(tgt, idx, src, axis=0):
    return tgt.at[idx].add(src)

def _segment_sum(src, seg, n):
    return jax.ops.segment_sum(src, seg, n)
kernel_name = 'mk_macaron_d1_jaxref_r8_a2231f'

def setup_inputs(seed: int=0):
    np.random.seed(seed)
    _w = jnp.asarray

    def _L0_attn_setup():
        import jax, jax.numpy as jnp
        import numpy as np
        B, T, D = (1, 256, 128)
        H, DH, DV, DF = (16, 64, 64, 512)
        EPS_LN = 1e-05
        EPS_DEN = 1e-06

        def _layernorm(x, g, b):
            m = jnp.mean(x, axis=-1, keepdims=True)
            v = jnp.mean((x - m) ** 2, axis=-1, keepdims=True)
            return (x - m) / jnp.sqrt(v + EPS_LN) * g + b

        def _phi(x):
            return jax.nn.elu(x) + 1.0

        def _linear_attention(x, Wq, Wk, Wv, Wo):
            b, t, d = x.shape
            Q = _phi((x @ Wq).reshape(b, t, H, DH)).transpose(0, 2, 1, 3)
            K = _phi((x @ Wk).reshape(b, t, H, DH)).transpose(0, 2, 1, 3)
            V = (x @ Wv).reshape(b, t, H, DV).transpose(0, 2, 1, 3)
            KV = jnp.einsum('bhti,bhtj->bhtij', K, V)
            S = jnp.cumsum(KV, axis=2)
            z = jnp.cumsum(K, axis=2)
            num = jnp.einsum('bhti,bhtij->bhtj', Q, S)
            den = jnp.maximum(jnp.einsum('bhti,bhti->bht', Q, z), EPS_DEN)[..., None]
            out = (num / den).transpose(0, 2, 1, 3).reshape(b, t, H * DV)
            return out @ Wo
        key = jax.random.key(seed)
        ks = jax.random.split(key, 8)
        s = 0.02
        return {'x': jax.random.normal(ks[0], (B, T, D), dtype=jnp.float32), 'ln1_g': jnp.ones((D,), jnp.float32), 'ln1_b': jnp.zeros((D,), jnp.float32), 'Wq': jax.random.normal(ks[1], (D, H * DH), jnp.float32) * s, 'Wk': jax.random.normal(ks[2], (D, H * DH), jnp.float32) * s, 'Wv': jax.random.normal(ks[3], (D, H * DV), jnp.float32) * s, 'Wo': jax.random.normal(ks[4], (H * DV, D), jnp.float32) * s, 'ln2_g': jnp.ones((D,), jnp.float32), 'ln2_b': jnp.zeros((D,), jnp.float32), 'Wf1': jax.random.normal(ks[5], (D, DF), jnp.float32) * s, 'Wf2': jax.random.normal(ks[6], (DF, D), jnp.float32) * s}
    _L0_attn_in = _L0_attn_setup()

    def _L0_ffn_setup():
        import jax, jax.numpy as jnp
        import numpy as np
        D_IN, D_HID = (128, 512)

        def _ternary(key, shape):
            return jax.random.randint(key, shape, -1, 2).astype(jnp.float32)

        def _tlin(x, w, s):
            return jnp.einsum('bsi,oi->bso', x, w) * s
        key = jax.random.key(seed)
        ks = jax.random.split(key, 12)
        inv = lambda fan: 1.0 / np.sqrt(fan).astype(np.float32)
        return {'x': jax.random.normal(ks[0], (4, 256, D_IN), dtype=jnp.float32), 'w1_w': _ternary(ks[1], (D_HID, D_IN)), 'w1_s': jax.random.uniform(ks[2], (D_HID,), dtype=jnp.float32) * inv(D_IN), 'w2_w': _ternary(ks[3], (D_HID, D_IN)), 'w2_s': jax.random.uniform(ks[4], (D_HID,), dtype=jnp.float32) * inv(D_IN), 'h1_w': _ternary(ks[5], (D_HID, D_HID)), 'h1_s': jax.random.uniform(ks[6], (D_HID,), dtype=jnp.float32) * inv(D_HID), 'h2_w': _ternary(ks[7], (D_HID, D_HID)), 'h2_s': jax.random.uniform(ks[8], (D_HID,), dtype=jnp.float32) * inv(D_HID), 'w3_w': _ternary(ks[9], (D_IN, D_HID)), 'w3_s': jax.random.uniform(ks[10], (D_IN,), dtype=jnp.float32) * inv(D_HID)}
    _L0_ffn_in = _L0_ffn_setup()
    _d = {'L0_attn_x': _L0_attn_in['x'], 'L0_attn_ln1_g': _L0_attn_in['ln1_g'], 'L0_attn_ln1_b': _L0_attn_in['ln1_b'], 'L0_attn_Wq': _L0_attn_in['Wq'], 'L0_attn_Wk': _L0_attn_in['Wk'], 'L0_attn_Wv': _L0_attn_in['Wv'], 'L0_attn_Wo': _L0_attn_in['Wo'], 'L0_attn_ln2_g': _L0_attn_in['ln2_g'], 'L0_attn_ln2_b': _L0_attn_in['ln2_b'], 'L0_attn_Wf1': _L0_attn_in['Wf1'], 'L0_attn_Wf2': _L0_attn_in['Wf2'], 'L0_ffn_w1_w': _L0_ffn_in['w1_w'], 'L0_ffn_w1_s': _L0_ffn_in['w1_s'], 'L0_ffn_w2_w': _L0_ffn_in['w2_w'], 'L0_ffn_w2_s': _L0_ffn_in['w2_s'], 'L0_ffn_h1_w': _L0_ffn_in['h1_w'], 'L0_ffn_h1_s': _L0_ffn_in['h1_s'], 'L0_ffn_h2_w': _L0_ffn_in['h2_w'], 'L0_ffn_h2_s': _L0_ffn_in['h2_s'], 'L0_ffn_w3_w': _L0_ffn_in['w3_w'], 'L0_ffn_w3_s': _L0_ffn_in['w3_s']}
    _x0 = _d['L0_attn_x']
    _d['L0_attn_x'] = jax.random.normal(jax.random.fold_in(jax.random.key(seed), 1), (4, 1024, 128), dtype=_x0.dtype)
    del _x0
    return _d

def reference(L0_attn_x, L0_attn_ln1_g, L0_attn_ln1_b, L0_attn_Wq, L0_attn_Wk, L0_attn_Wv, L0_attn_Wo, L0_attn_ln2_g, L0_attn_ln2_b, L0_attn_Wf1, L0_attn_Wf2, L0_ffn_w1_w, L0_ffn_w1_s, L0_ffn_w2_w, L0_ffn_w2_s, L0_ffn_h1_w, L0_ffn_h1_s, L0_ffn_h2_w, L0_ffn_h2_s, L0_ffn_w3_w, L0_ffn_w3_s):

    def _L0_attn_ref(x, ln1_g, ln1_b, Wq, Wk, Wv, Wo, ln2_g, ln2_b, Wf1, Wf2):
        import jax, jax.numpy as jnp
        import numpy as np
        B, T, D = (1, 256, 128)
        H, DH, DV, DF = (16, 64, 64, 512)
        EPS_LN = 1e-05
        EPS_DEN = 1e-06

        def _layernorm(x, g, b):
            m = jnp.mean(x, axis=-1, keepdims=True)
            v = jnp.mean((x - m) ** 2, axis=-1, keepdims=True)
            return (x - m) / jnp.sqrt(v + EPS_LN) * g + b

        def _phi(x):
            return jax.nn.elu(x) + 1.0

        def _linear_attention(x, Wq, Wk, Wv, Wo):
            b, t, d = x.shape
            Q = _phi((x @ Wq).reshape(b, t, H, DH)).transpose(0, 2, 1, 3)
            K = _phi((x @ Wk).reshape(b, t, H, DH)).transpose(0, 2, 1, 3)
            V = (x @ Wv).reshape(b, t, H, DV).transpose(0, 2, 1, 3)
            KV = jnp.einsum('bhti,bhtj->bhtij', K, V)
            S = jnp.cumsum(KV, axis=2)
            z = jnp.cumsum(K, axis=2)
            num = jnp.einsum('bhti,bhtij->bhtj', Q, S)
            den = jnp.maximum(jnp.einsum('bhti,bhti->bht', Q, z), EPS_DEN)[..., None]
            out = (num / den).transpose(0, 2, 1, 3).reshape(b, t, H * DV)
            return out @ Wo
        x = x + _linear_attention(_layernorm(x, ln1_g, ln1_b), Wq, Wk, Wv, Wo)
        h = _layernorm(x, ln2_g, ln2_b)
        x = x + jax.nn.gelu(h @ Wf1, approximate=False) @ Wf2
        return x

    def _L0_ffn_ref(x, w1_w, w1_s, w2_w, w2_s, h1_w, h1_s, h2_w, h2_s, w3_w, w3_s):
        import jax, jax.numpy as jnp
        import numpy as np
        D_IN, D_HID = (128, 512)

        def _ternary(key, shape):
            return jax.random.randint(key, shape, -1, 2).astype(jnp.float32)

        def _tlin(x, w, s):
            return jnp.einsum('bsi,oi->bso', x, w) * s
        h = jax.nn.silu(_tlin(x, w1_w, w1_s)) * _tlin(x, w2_w, w2_s)
        h = jax.nn.gelu(_tlin(h, h1_w, h1_s), approximate=False)
        h = jax.nn.gelu(_tlin(h, h2_w, h2_s), approximate=False)
        return _tlin(h, w3_w, w3_s)
    x = L0_attn_x
    x = x + 0.5 * _L0_ffn_ref(_layernorm(x, axis=-1), L0_ffn_w1_w, L0_ffn_w1_s, L0_ffn_w2_w, L0_ffn_w2_s, L0_ffn_h1_w, L0_ffn_h1_s, L0_ffn_h2_w, L0_ffn_h2_s, L0_ffn_w3_w, L0_ffn_w3_s)
    x = x + _L0_attn_ref(_layernorm(x, axis=-1), L0_attn_ln1_g, L0_attn_ln1_b, L0_attn_Wq, L0_attn_Wk, L0_attn_Wv, L0_attn_Wo, L0_attn_ln2_g, L0_attn_ln2_b, L0_attn_Wf1, L0_attn_Wf2)
    x = x + 0.5 * _L0_ffn_ref(_layernorm(x, axis=-1), L0_ffn_w1_w, L0_ffn_w1_s, L0_ffn_w2_w, L0_ffn_w2_s, L0_ffn_h1_w, L0_ffn_h1_s, L0_ffn_h2_w, L0_ffn_h2_s, L0_ffn_w3_w, L0_ffn_w3_s)
    return x

_drawn_inputs = setup_inputs


def setup_inputs(seed=0):
    import zlib

    import numpy as np

    out = dict(_drawn_inputs(seed))
    spreads = {'L0_attn_ln1_g': (1.0, 0.2),
     'L0_attn_ln1_b': (0.0, 0.1),
     'L0_attn_ln2_g': (1.0, 0.2),
     'L0_attn_ln2_b': (0.0, 0.1)}
    factors = {}
    for name, (base, spread) in spreads.items():
        noise = np.random.default_rng([zlib.crc32(name.encode()), seed]).standard_normal(out[name].shape)
        drawn = base * np.exp(spread * noise) if base else spread * noise
        out[name] = jnp.asarray(drawn.astype(out[name].dtype))
    for name, factor in factors.items():
        out[name] = (out[name] * factor).astype(out[name].dtype)
    return out
```

```python
from contextlib import ExitStack

import concourse.bass as bass
from concourse import mybir

P = 128
ALU = mybir.AluOpType
ACT = mybir.ActivationFunctionType
F32 = mybir.dt.float32
F32R = mybir.dt.float32r
EPS_LN = 1e-5
EPS_DEN = 1e-6

TILE = 512
Q = TILE // P
PAIR = ("A", "B")


class Steps:

    def __init__(self, sem, base, names):
        assert len(set(names)) == len(names)
        self.sem, self.base, self.names = sem, base, names
        self.at = {name: n + 1 for n, name in enumerate(names)}
        self.next = 0

    def step(self, name):
        assert self.names[self.next % len(self.names)] == name, (name, self.names[self.next % len(self.names)])
        self.next += 1
        return self.sem, 1

    def done(self, name, i, back=0):
        return self.sem, i * len(self.names) + (self.base + self.at[name] - back * len(self.names))

    def end(self, iterations):
        return self.base + iterations * len(self.names)


class Banks:

    def __init__(self, jobs):
        self.bank = {job: bank for job, bank, _, _ in jobs}
        self.prior = {}
        for n, (job, bank, _, _) in enumerate(jobs):
            same = [k for k, j in enumerate(jobs) if j[1] == bank]
            before = [k for k in same if k < n]
            k = before[-1] if before else same[-1]
            self.prior[job] = (jobs[k][2], jobs[k][3], 0 if before else 1)

    def emptied(self, job, i):
        steps, name, back = self.prior[job]
        return steps.done(name, i, back)


def build_kernel(nc, t, out):
    x_in = t["L0_attn_x"].rearrange("b t d -> (b t) d")
    NTOK, D = x_in.shape
    DH_ = t["L0_ffn_h1_w"].shape[0]
    KT = DH_ // P
    DA = t["L0_attn_Wq"].shape[1]
    DH = 64
    H = DA // DH
    PR = H // 2
    NB = t["L0_attn_x"].shape[0]
    NT = NTOK // TILE
    NI = NT // 2
    SUP = NT // NB
    HW = DH + 2
    PW = 2 * HW
    OG = [(0, 3), (3, 6), (6, 8)]
    assert D == P and NTOK % (2 * TILE) == 0 and H == 16 and KT == 4 and t["L0_attn_Wf1"].shape[1] == DH_

    W1, W2, H1, H2, W3 = 0, DH_, 2 * DH_, 2 * DH_ + KT * DH_, 2 * DH_ + 2 * KT * DH_
    WCOLS = W3 + DH_

    ctx = ExitStack()

    def sem(name):
        return ctx.enter_context(nc.semaphore(name))

    def sb(stack, name, shape, dt=F32):
        return stack.enter_context(nc.sbuf_tensor(name, shape, dt))

    def view(dram):
        return dram.rearrange("(n q p) d -> n p q d", q=Q, p=P)

    with ctx:
        ident = sb(ctx, "ident", [P, P])
        mask = sb(ctx, "mask", [P, 4, P])
        wh = sb(ctx, "wh", [P, WCOLS], F32R)
        wl = sb(ctx, "wl", [P, WCOLS], F32R)
        fh = sb(ctx, "fh", [P, 2 * DH_], F32R)
        fl = sb(ctx, "fl", [P, 2 * DH_], F32R)
        wq = sb(ctx, "wq", [P, DA])
        wk = sb(ctx, "wk", [P, DA])
        wv = sb(ctx, "wv", [P, DA])
        wo = sb(ctx, "wo", [P, PR, D])
        NV = 4 * KT + 5
        sc = sb(ctx, "sc", [P, NV])
        s3 = sb(ctx, "s3", [P, 1])
        affine = sc[:, NV - 4:NV]
        spare = sb(ctx, "spare", [P, 5])
        power = sb(ctx, "power", [P, Q])
        x1_d = nc.dram_tensor("x1_scratch", (NTOK, D), F32).ap()
        y_d = nc.dram_tensor("y_scratch", (NTOK, D), F32).ap()
        xs_d = nc.dram_tensor("xs_scratch", (NTOK, D), F32).ap()
        x2_d = nc.dram_tensor("x2_scratch", (NTOK, D), F32).ap()
        ps = [ctx.enter_context(nc.psum_tensor(f"ps{b}", [P, TILE], F32)) for b in range(8)]

        with ExitStack() as s:
            st1 = sb(s, "st1", [P, KT, D])
            st2 = sb(s, "st2", [P, KT, D])
            sh1 = sb(s, "sh1", [P, KT, DH_])
            sh2 = sb(s, "sh2", [P, KT, DH_])
            st3 = sb(s, "st3", [P, DH_])
            sf = sb(s, "sf", [P, 2 * DH_])
            vec = sb(s, "vec", [NV, P])

        with ExitStack() as s:
            xln = [sb(s, f"xln{u}", [P, Q, D]) for u in PAIR]
            xres = [sb(s, f"xres{u}", [P, Q, D]) for u in PAIR]
            xn = [sb(s, f"xn{u}", [P, Q, D]) for u in PAIR]
            nh = [sb(s, f"nh{u}", [P, TILE], F32R) for u in PAIR]
            nl = [sb(s, f"nl{u}", [P, TILE], F32R) for u in PAIR]
            ah = [[sb(s, f"ah{u}{k}", [P, KT, TILE], F32R) for k in range(2)] for u in PAIR]
            al = [[sb(s, f"al{u}{k}", [P, KT, TILE], F32R) for k in range(2)] for u in PAIR]
            NF = 6
            full = [sb(s, f"full{k}", [P, TILE]) for k in range(NF)]
            NS = 3
            gate = [sb(s, f"gate{k}", [P, TILE]) for k in range(NS)]
            yf = [sb(s, f"yf{u}", [P, TILE]) for u in PAIR]
            xo = [sb(s, f"xo{u}", [P, Q, D]) for u in PAIR]
            bst = [sb(s, f"bst{u}", [P, Q, 6]) for u in PAIR]
            bag = [sb(s, f"bag{u}", [P, Q, 2]) for u in PAIR]
            ve = [sb(s, f"ve{u}", [P, Q]) for u in PAIR]
            rs = [sb(s, f"rs{u}", [P, Q]) for u in PAIR]

        with ExitStack() as s:
            ax = sb(s, "ax", [P, Q, D])
            axp = sb(s, "axp", [P, Q, D])
            axn = sb(s, "axn", [P, Q, D])
            ahn = sb(s, "ahn", [P, TILE])
            qf = sb(s, "qf", [P, PR, TILE])
            kt_ = [sb(s, f"kt{k}", [P, DA]) for k in range(2)]
            vt = [sb(s, f"vt{k}", [P, H, HW]) for k in range(2)]
            kf = [sb(s, f"kf{k}", [P, PR, P]) for k in range(2)]
            am = [sb(s, f"am{k}", [P, 4, 4, P]) for k in range(2)]
            state = sb(s, "state", [P, PR, PW])
            ot = [sb(s, f"ot{k}", [P, H, DH]) for k in range(2)]
            of = sb(s, "of", [P, PR, TILE])
            NE = 3
            ee = [sb(s, f"ee{k}", [P, TILE]) for k in range(NE)]
            rr = [sb(s, f"rr{k}", [P, TILE]) for k in range(NE)]
            den = [sb(s, f"den{k}", [P, 6]) for k in range(2)]
            rden = [sb(s, f"rden{k}", [P, 6]) for k in range(2)]
            ayf = sb(s, "ayf", [P, TILE])
            ay = sb(s, "ay", [P, Q, D])
            axs = sb(s, "axs", [P, Q, D])
            abst = sb(s, "abst", [P, Q, 6])
            abag = sb(s, "abag", [P, Q, 2])
            av = sb(s, "av", [P, Q])
            ar1 = sb(s, "ar1", [P, Q])
            av1 = sb(s, "av1", [P, Q])
            av2 = sb(s, "av2", [P, Q])
            av3 = sb(s, "av3", [P, Q])
            ar2 = sb(s, "ar2", [P, Q])

        pe_did, act_did, dve_did, pool_did = sem("pe_did"), sem("act_did"), sem("dve_did"), sem("pool_did")
        in_w, in_wt, in_v = sem("in_w"), sem("in_wt"), sem("in_v")
        in_ln = [sem(f"in_ln{u}") for u in PAIR]
        in_res = [sem(f"in_res{u}") for u in PAIR]
        out_x = [sem(f"out_x{u}") for u in PAIR]
        in_ax, out_y, out_xs = sem("in_ax"), sem("out_y"), sem("out_xs")

        PRIME = 256
        ENG = ("pe", "act", "dve", "pool")
        sems = dict(pe=pe_did, act=act_did, dve=dve_did, pool=pool_did)
        base = dict.fromkeys(ENG, PRIME)
        plan = []

        def phase(iterations, **names):
            steps = {e: Steps(sems[e], base[e], names.get(e, [])) for e in ENG}
            for e in ENG:
                base[e] = steps[e].end(iterations)
            plan.append(steps)
            return steps

        def all_before(eng, steps):
            for e in ENG:
                eng.wait_ge(steps[e].sem, steps[e].base)

        groups = ([(W1, [st1[:, m, :] for m in range(KT)])] + [(W2, [st2[:, m, :] for m in range(KT)])]
                  + [(H1 + k * DH_, [sh1[:, m, k * P:(k + 1) * P] for m in range(KT)]) for k in range(KT)]
                  + [(H2 + k * DH_, [sh2[:, m, k * P:(k + 1) * P] for m in range(KT)]) for k in range(KT)]
                  + [(W3, [st3[:, k * P:(k + 1) * P] for k in range(KT)])])
        NG = len(groups)
        setup = phase(1, pe=["vT"] + [f"wT{g}" for g in range(NG)],
                      dve=["prime", "vec", "const"] + [f"{w}{g}" for g in range(NG) for w in ("hi", "lo")]
                      + ["fhi", "flo"],
                      pool=["ones", "ident", "mask1", "mask"])

        LAYERS = {"ternary": ["L1", "H1", "H2", "W3"], "plain": ["L1", "W3"]}

        def ffn_plan(kind):
            tern = kind == "ternary"
            pe, act, dve, pool, splits, gates = [], [], [], [], [], []

            def split(name):
                splits.append(name)
                dve.append(f"hi_{name}")
                pool.append(f"lo_{name}")

            def layer(name, u):
                for m in range(KT):
                    if name == "L1" and tern:
                        pe.extend([f"g{u}{m}", f"v{u}{m}"])
                        act.append(f"silu{u}{m}")
                        gates.append(f"{u}{m}")
                        dve.append(f"mul{u}{m}")
                    else:
                        pe.append(f"{name}{u}{m}")
                        act.append(f"gelu_{name}{u}{m}")
                    split(f"{name}{u}{m}")

            def stats(u):
                dve.extend([f"st{u}", f"ag{u}", f"ve{u}", f"xn{u}"])
                pool.append(f"rs{u}")

            def norm(u):
                pe.append(f"nT{u}")
                act.append(f"hf{u}")
                split(f"n{u}")

            seq = LAYERS[kind]
            layer(seq[0], "A")
            stats("A")
            layer(seq[0], "B")
            stats("B")
            norm("A")
            for k, name in enumerate(seq[1:-1]):
                layer(name, "A")
                if k == 0:
                    norm("B")
                layer(name, "B")
            pe.append("W3A")
            act.append("yA")
            if not tern:
                norm("B")
            pe.extend(["W3B", "yTA", "yTB"])
            act.append("yB")
            dve.extend(["resA", "resB"])
            pro_dve = [f"{n}{u}" for u in PAIR for n in ("st", "ag", "ve", "xn")] + [f"hi_n{u}" for u in PAIR]
            pro_pool = [f"rs{u}" for u in PAIR] + [f"lo_n{u}" for u in PAIR]
            pro = phase(1, pe=["nTA", "nTB"], act=["hfA", "hfB"], dve=pro_dve, pool=pro_pool)
            loop = phase(NI, pe=pe, act=act, dve=dve, pool=pool)
            A, V = loop["act"], loop["dve"]
            jobs, n = [], 0
            for name in pe:
                if name[:2] == "nT":
                    jobs.append((name, 6, A, "hf" + name[2]))
                elif name[:2] == "yT":
                    jobs.append((name, 7, V, "res" + name[2]))
                else:
                    if name[:2] == "W3":
                        by = (A, "y" + name[2])
                    elif name[0] == "g":
                        by = (A, "silu" + name[1:])
                    elif name[0] == "v":
                        by = (V, "mul" + name[1:])
                    else:
                        by = (A, "gelu_" + name)
                    jobs.append((name, n % 6, *by))
                    n += 1
            return dict(kind=kind, pro=pro, loop=loop, banks=Banks(jobs), splits=splits, gates=gates)

        ffn1 = ffn_plan("ternary")

        C = range(Q)
        SG = ("a0", "b0", "a1", "b1")

        def attention_plan():
            pe, act, dve, pool, phis = [], [], [], [], []
            jobs, n_p, n_o = [], [0], [0]

            def p_job(name, eng, by):
                pe.append(name)
                jobs.append((name, n_p[0] % 2, eng, by))
                n_p[0] += 1

            def o_job(name, eng, by):
                pe.append(name)
                jobs.append((name, 6 + n_o[0] % 2, eng, by))
                n_o[0] += 1

            def phi(name):
                phis.append(name)
                p_job(name, "act", f"r_{name}")
                act.extend([f"e_{name}", f"r_{name}"])
                dve.append(f"phi_{name}")

            def kv(c):
                for h in range(2):
                    phi(f"K{c}{h}")
                for h in range(2):
                    p_job(f"V{c}{h}", "act", f"v{c}{h}")
                    act.append(f"v{c}{h}")

            dve.extend(["st", "ag", "ve", "v1", "v2", "v3", "xp", "xn"])
            pool.extend(["r1", "r2"])
            p_job("nT", "act", "hf")
            act.append("hf")
            for p in range(PR):
                phi(f"Q{p}")
            kv(0)
            for c in C:
                for j in range(2):
                    p_job(f"KT{c}{j}", "act", f"kt{c}{j}")
                    act.append(f"kt{c}{j}")
                for k, g in enumerate(SG):
                    jobs.append((f"S{c}{g}", 2 + k, "dve", f"am{c}{g}"))
                    dve.append(f"am{c}{g}")
                pe.extend([f"S{c}a0", f"S{c}b0", f"S{c}a1", f"S{c}b1"])
                if c + 1 < Q:
                    kv(c + 1)
                for g in range(3):
                    o_job(f"O{c}{g}", "dve", f"on{c}{g}")
                    dve.extend([f"dm{c}{g}", f"rd{c}{g}", f"on{c}{g}"])
                for g in range(3):
                    o_job(f"D{c}{g}", "dve", f"sb{c}{g}")
                    dve.extend([f"sa{c}{g}", f"sb{c}{g}"])
                for j in range(2):
                    p_job(f"OT{c}{j}", "act", f"ot{c}{j}")
                    act.append(f"ot{c}{j}")
            p_job("WO", "act", "wf")
            act.append("wf")
            p_job("yT", "dve", "y")
            dve.extend(["y", "ys"])
            loop = phase(NT, pe=pe, act=act, dve=dve, pool=pool)
            return dict(loop=loop, banks=Banks([(j, b, loop[e], by) for j, b, e, by in jobs]), phis=phis)

        attn = attention_plan()
        ffn2 = ffn_plan("plain")
        ffn3 = ffn_plan("ternary")
        ffn1.update(n=0, ln=x_in, res=x_in, dst=x1_d, hi=wh, lo=wl, gain=None)
        ffn2.update(n=1, ln=y_d, res=xs_d, dst=x2_d, hi=fh, lo=fl, gain=(affine[:, 2:3], affine[:, 3:4]))
        ffn3.update(n=2, ln=x2_d, res=x2_d, dst=out, hi=wh, lo=wl, gain=None)

        block = ctx.enter_context(nc.Block())

        @block.sync
        def _(sp):
            for dst, name in ((st1, "w1"), (st2, "w2"), (sh1, "h1"), (sh2, "h2")):
                sp.dma_start(dst[:, :, :], t[f"L0_ffn_{name}_w"].rearrange("(m p) i -> p m i", p=P)).then_inc(in_wt, 16)
            sp.dma_start(st3[:, :], t["L0_ffn_w3_w"]).then_inc(in_wt, 16)
            sp.dma_start(sf[:, 0:DH_], t["L0_attn_Wf1"]).then_inc(in_w, 16)
            sp.dma_start(sf[:, DH_:2 * DH_].rearrange("p (k n) -> p k n", k=KT),
                         t["L0_attn_Wf2"].rearrange("(k p) n -> p k n", p=P)).then_inc(in_w, 16)
            for k, name in enumerate(("w1", "w2", "h1", "h2")):
                sp.dma_start(vec[k * KT:(k + 1) * KT, :],
                             t[f"L0_ffn_{name}_s"].rearrange("(m p) -> m p", p=P)).then_inc(in_v, 16)
            sp.dma_start(vec[4 * KT:4 * KT + 1, :], t["L0_ffn_w3_s"].rearrange("(a p) -> a p", a=1)).then_inc(in_v, 16)
            for k, name in enumerate(("ln1_g", "ln1_b", "ln2_g", "ln2_b")):
                sp.dma_start(vec[4 * KT + 1 + k:4 * KT + 2 + k, :],
                             t[f"L0_attn_{name}"].rearrange("(a p) -> a p", a=1)).then_inc(in_v, 16)
            for dst, name in ((wq, "Wq"), (wk, "Wk"), (wv, "Wv")):
                sp.dma_start(dst[:, :], t[f"L0_attn_{name}"]).then_inc(in_w, 16)
            sp.dma_start(wo[:, :, :], t["L0_attn_Wo"].rearrange("(k p) n -> p k n", p=P)).then_inc(in_w, 16)

            def ffn_dma(f):
                n, V, PV = f["n"], f["loop"]["dve"], f["pro"]["dve"]
                src, res, dst = view(f["ln"]), view(f["res"]), view(f["dst"])
                all_before(sp, f["pro"])
                for u in range(2):
                    sp.dma_start(xln[u][:, :, :], src[u]).then_inc(in_ln[u], 16)
                all_before(sp, f["loop"])
                with sp.Fori(0, NI) as i:
                    for u, U in enumerate(PAIR):
                        sp.wait_ge(*V.done(f"xn{U}", i, 1))
                        sp.dma_start(xln[u][:, :, :], src[((i + 1) % NI) * 2 + u]).then_inc(in_ln[u], 16)
                        sp.wait_ge(*V.done(f"res{U}", i, 1))
                        sp.dma_start(xres[u][:, :, :], res[i * 2 + u]).then_inc(in_res[u], 16)
                    for u, U in enumerate(PAIR):
                        sp.wait_ge(*V.done(f"res{U}", i))
                        sp.dma_start(dst[i * 2 + u], xo[u][:, :, :]).then_inc(out_x[u], 16)
                for u in range(2):
                    sp.wait_ge(out_x[u], 16 * NI * (n + 1) + 16)

            ffn_dma(ffn1)

            V = attn["loop"]["dve"]
            all_before(sp, attn["loop"])
            with sp.Fori(0, NT) as i:
                sp.wait_ge(*V.done("ys", i, 1))
                sp.dma_start(ax[:, :, :], view(x1_d)[i]).then_inc(in_ax, 16)
                sp.wait_ge(*V.done("y", i))
                sp.dma_start(view(y_d)[i], ay[:, :, :]).then_inc(out_y, 16)
                sp.wait_ge(*V.done("ys", i))
                sp.dma_start(view(xs_d)[i], axs[:, :, :]).then_inc(out_xs, 16)
            sp.wait_ge(out_y, 16 * NT + 16)
            sp.wait_ge(out_xs, 16 * NT + 16)

            ffn_dma(ffn2)
            ffn_dma(ffn3)

        @block.tensor
        def _(pe):
            def transposes(dst, sources, steps, name):
                for k, src in enumerate(sources):
                    ins = nc.tensor.transpose(dst[:, k * P:(k + 1) * P], src, ident[:, :])
                ins.then_inc(*steps.step(name))

            S = setup
            pe.wait_ge(*S["pool"].done("ident", 0))
            pe.wait_ge(in_v, 9 * 16)
            nc.tensor.transpose(ps[7][:, 0:NV], vec[:, :], ident[0:NV, 0:NV]).then_inc(*S["pe"].step("vT"))
            pe.wait_ge(in_wt, 5 * 16)
            for g, (_, sources) in enumerate(groups):
                if g == 7:
                    pe.wait_ge(*S["dve"].done("vec", 0))
                if g >= 8:
                    pe.wait_ge(*S["dve"].done(f"lo{g - 8}", 0))
                transposes(ps[g % 8], sources, S["pe"], f"wT{g}")

            def ffn_pe(f):
                kind, banks, L = f["kind"], f["banks"], f["loop"]
                G = f["pro"]
                all_before(pe, G)
                for u, U in enumerate(PAIR):
                    pe.wait_ge(*G["dve"].done(f"xn{U}", 0))
                    transposes(ps[u], [xn[u][:, q, :] for q in range(Q)], G["pe"], f"nT{U}")
                all_before(pe, L)

                def product(name, i, col, hi_in, lo_in, ks):
                    pe.wait_ge(*banks.emptied(name, i))
                    b = ps[banks.bank[name]]
                    parts = [(k, xp_, w) for k in ks for xp_, w in ((hi_in, f["hi"]), (lo_in, f["hi"]), (hi_in, f["lo"]))]
                    for n, (k, x_, w) in enumerate(parts):
                        ins = nc.tensor.matmul(b[:, :], w[:, col(k):col(k) + P], x_[:, k, :],
                                               start=(n == 0), stop=(n == len(parts) - 1))
                    ins.then_inc(*L["pe"].step(name))

                def norm(u, U, i):
                    pe.wait_ge(*L["dve"].done(f"xn{U}", i))
                    pe.wait_ge(*banks.emptied(f"nT{U}", i))
                    transposes(ps[banks.bank[f"nT{U}"]], [xn[u][:, q, :] for q in range(Q)], L["pe"], f"nT{U}")

                def first(u, U, i):
                    hi_in, lo_in = (a[u][:, :].rearrange("p (k n) -> p k n", k=1) for a in (nh, nl))
                    pe.wait_ge(*L["pool"].done(f"lo_n{U}", i, 1))
                    for m in range(KT):
                        if kind == "ternary":
                            product(f"g{U}{m}", i, lambda k: W1 + m * P, hi_in, lo_in, [0])
                            product(f"v{U}{m}", i, lambda k: W2 + m * P, hi_in, lo_in, [0])
                        else:
                            product(f"L1{U}{m}", i, lambda k: m * P, hi_in, lo_in, [0])

                def hidden(name, before, off, src, u, U, i):
                    pe.wait_ge(*L["pool"].done(f"lo_{before}{U}{KT - 1}", i))
                    for m in range(KT):
                        product(f"{name}{U}{m}", i, lambda k: off + k * DH_ + m * P, ah[u][src], al[u][src], range(KT))

                def last(before, off, src, u, U, i):
                    pe.wait_ge(*L["pool"].done(f"lo_{before}{U}{KT - 1}", i))
                    product(f"W3{U}", i, lambda k: off + k * P, ah[u][src], al[u][src], range(KT))

                with pe.Fori(0, NI) as i:
                    first(0, "A", i)
                    first(1, "B", i)
                    norm(0, "A", i)
                    if kind == "ternary":
                        hidden("H1", "L1", H1, 0, 0, "A", i)
                        norm(1, "B", i)
                        hidden("H1", "L1", H1, 0, 1, "B", i)
                        hidden("H2", "H1", H2, 1, 0, "A", i)
                        hidden("H2", "H1", H2, 1, 1, "B", i)
                        last("H2", W3, 0, 0, "A", i)
                        last("H2", W3, 0, 1, "B", i)
                    else:
                        last("L1", DH_, 0, 0, "A", i)
                        norm(1, "B", i)
                        last("L1", DH_, 0, 1, "B", i)
                    for u, U in enumerate(PAIR):
                        pe.wait_ge(*L["act"].done(f"y{U}", i))
                        pe.wait_ge(*banks.emptied(f"yT{U}", i))
                        transposes(ps[banks.bank[f"yT{U}"]], [yf[u][:, q * P:(q + 1) * P] for q in range(Q)],
                                   L["pe"], f"yT{U}")

            ffn_pe(ffn1)

            L, banks = attn["loop"], attn["banks"]
            all_before(pe, L)
            pe.wait_ge(in_w, 6 * 16)

            def bank(name, i):
                pe.wait_ge(*banks.emptied(name, i))
                return ps[banks.bank[name]]

            def keys_values(c, i):
                lhs = ahn[:, c * P:(c + 1) * P]
                for w, kind in ((wk, "K"), (wv, "V")):
                    for h in range(2):
                        b = bank(f"{kind}{c}{h}", i)
                        nc.tensor.matmul(b[:, :], lhs, w[:, h * TILE:(h + 1) * TILE], start=True, stop=True)\
                            .then_inc(*L["pe"].step(f"{kind}{c}{h}"))

            with pe.Fori(0, NT) as i:
                pe.wait_ge(*L["dve"].done("xn", i))
                transposes(bank("nT", i), [axn[:, q, :] for q in range(Q)], L["pe"], "nT")
                pe.wait_ge(*L["act"].done("hf", i))
                for p in range(PR):
                    b = bank(f"Q{p}", i)
                    nc.tensor.matmul(b[:, :], wq[:, p * P:(p + 1) * P], ahn[:, :], start=True, stop=True)\
                        .then_inc(*L["pe"].step(f"Q{p}"))
                keys_values(0, i)
                for c in C:
                    k = c % 2
                    own = slice(c * P, (c + 1) * P)
                    for j in range(2):
                        pe.wait_ge(*L["dve"].done(f"phi_K{c}{j}", i))
                        transposes(bank(f"KT{c}{j}", i), [kt_[k][:, (4 * j + n) * P:(4 * j + n + 1) * P] for n in range(4)],
                                   L["pe"], f"KT{c}{j}")
                    pe.wait_ge(*L["dve"].done(f"phi_Q{PR - 1}", i))
                    for j in range(2):
                        pe.wait_ge(*L["act"].done(f"kt{c}{j}", i))
                        ba, bb = bank(f"S{c}a{j}", i), bank(f"S{c}b{j}", i)
                        for n in range(4):
                            p = 4 * j + n
                            ia = nc.tensor.matmul(ba[:, n * P:(n + 1) * P], kf[k][0:DH, p, :], qf[0:DH, p, own],
                                                  start=True, stop=True)
                            ib = nc.tensor.matmul(bb[:, n * P:(n + 1) * P], kf[k][DH:P, p, :], qf[DH:P, p, own],
                                                  start=True, stop=True)
                            if n == 3:
                                ia.then_inc(*L["pe"].step(f"S{c}a{j}"))
                                ib.then_inc(*L["pe"].step(f"S{c}b{j}"))
                    if c + 1 < Q:
                        keys_values(c + 1, i)
                    pe.wait_ge(*L["act"].done(f"v{c}1", i))
                    if c:
                        pe.wait_ge(*L["dve"].done(f"sb{c - 1}2", i))
                    else:
                        pe.wait_ge(*L["dve"].done("st", i))
                    pe.wait_ge(*L["dve"].done(f"am{c}b1", i))
                    for g, (p0, p1) in enumerate(OG):
                        b = bank(f"O{c}{g}", i)
                        for p in range(p0, p1):
                            o = (p - p0) * PW
                            nc.tensor.matmul(b[:, o:o + PW], qf[:, p, own], state[:, p, :], start=True, stop=False)
                            for n in range(2):
                                ins = nc.tensor.matmul(b[:, o + n * HW:o + (n + 1) * HW], am[k][:, 2 * (p // 4) + n, p % 4, :],
                                                       vt[k][:, 2 * p + n, :], start=False, stop=(n == 1))
                        ins.then_inc(*L["pe"].step(f"O{c}{g}"))
                    for g, (p0, p1) in enumerate(OG):
                        b = bank(f"D{c}{g}", i)
                        for p in range(p0, p1):
                            o = (p - p0) * PW
                            ins = nc.tensor.matmul(b[:, o:o + PW], kt_[k][:, p * P:(p + 1) * P],
                                                   vt[k][:, 2 * p:2 * p + 2, :], start=True, stop=True)
                        ins.then_inc(*L["pe"].step(f"D{c}{g}"))
                    pe.wait_ge(*L["dve"].done(f"on{c}2", i))
                    for j in range(2):
                        b = bank(f"OT{c}{j}", i)
                        transposes(b, [ot[k][:, 2 * p:2 * p + 2, :] for p in range(4 * j, 4 * j + 4)],
                                   L["pe"], f"OT{c}{j}")
                pe.wait_ge(*L["act"].done(f"ot{Q - 1}1", i))
                b = bank("WO", i)
                for p in range(PR):
                    ins = nc.tensor.matmul(b[:, :], wo[:, p, :], of[:, p, :], start=(p == 0), stop=(p == PR - 1))
                ins.then_inc(*L["pe"].step("WO"))
                pe.wait_ge(*L["act"].done("wf", i))
                transposes(bank("yT", i), [ayf[:, q * P:(q + 1) * P] for q in range(Q)], L["pe"], "yT")

            ffn_pe(ffn2)
            ffn_pe(ffn3)

        @block.scalar
        def _(act):
            def ffn_act(f):
                G, L = f["pro"], f["loop"]
                tern = f["kind"] == "ternary"

                def slot(name):
                    return full[f["splits"].index(name) % NF]

                def slot_free(name, i):
                    k = f["splits"].index(name)
                    if k >= NF:
                        act.wait_ge(*L["pool"].done("lo_" + f["splits"][k - NF], i))
                    else:
                        last = max(j for j in range(len(f["splits"])) if j % NF == k)
                        act.wait_ge(*L["pool"].done("lo_" + f["splits"][last], i, 1))

                def normalised(dst, src):
                    if f["gain"]:
                        return nc.scalar.activation(dst, src, ACT.Identity, scale=f["gain"][0], bias=f["gain"][1])
                    return nc.scalar.copy(dst, src)

                all_before(act, G)
                for u, U in enumerate(PAIR):
                    act.wait_ge(*G["pe"].done(f"nT{U}", 0))
                    normalised(full[u][:, :], ps[u][:, :]).then_inc(*G["act"].step(f"hf{U}"))
                all_before(act, L)

                def norm(u, U, i):
                    act.wait_ge(*L["pe"].done(f"nT{U}", i))
                    slot_free(f"n{U}", i)
                    normalised(slot(f"n{U}")[:, :], ps[f["banks"].bank[f"nT{U}"]][:, :]).then_inc(*L["act"].step(f"hf{U}"))

                def silu(U, i):
                    for m in range(KT):
                        k = f["gates"].index(f"{U}{m}")
                        act.wait_ge(*L["pe"].done(f"g{U}{m}", i))
                        if k >= NS:
                            act.wait_ge(*L["dve"].done("mul" + f["gates"][k - NS], i))
                        else:
                            last = max(j for j in range(len(f["gates"])) if j % NS == k)
                            act.wait_ge(*L["dve"].done("mul" + f["gates"][last], i, 1))
                        nc.scalar.activation(gate[k % NS][:, :], ps[f["banks"].bank[f"g{U}{m}"]][:, :], ACT.Silu,
                                             scale=sc[:, m:m + 1]).then_inc(*L["act"].step(f"silu{U}{m}"))

                def gelu(name, scale, U, i):
                    for m in range(KT):
                        act.wait_ge(*L["pe"].done(f"{name}{U}{m}", i))
                        slot_free(f"{name}{U}{m}", i)
                        s_ = sc[:, scale + m:scale + m + 1] if scale is not None else 1.0
                        nc.scalar.activation(slot(f"{name}{U}{m}")[:, :], ps[f["banks"].bank[f"{name}{U}{m}"]][:, :],
                                             ACT.Gelu, scale=s_).then_inc(*L["act"].step(f"gelu_{name}{U}{m}"))

                def evacuate(u, U, i):
                    act.wait_ge(*L["pe"].done(f"W3{U}", i))
                    act.wait_ge(*L["pe"].done(f"yT{U}", i, 1))
                    nc.scalar.activation(yf[u][:, :], ps[f["banks"].bank[f"W3{U}"]][:, :], ACT.Identity,
                                         scale=s3[:, 0:1] if tern else 1.0).then_inc(*L["act"].step(f"y{U}"))

                with act.Fori(0, NI) as i:
                    if tern:
                        silu("A", i)
                        silu("B", i)
                        norm(0, "A", i)
                        gelu("H1", 2 * KT, "A", i)
                        norm(1, "B", i)
                        gelu("H1", 2 * KT, "B", i)
                        gelu("H2", 3 * KT, "A", i)
                        gelu("H2", 3 * KT, "B", i)
                        evacuate(0, "A", i)
                    else:
                        gelu("L1", None, "A", i)
                        gelu("L1", None, "B", i)
                        norm(0, "A", i)
                        evacuate(0, "A", i)
                        norm(1, "B", i)
                    evacuate(1, "B", i)

            ffn_act(ffn1)

            L, banks, phis = attn["loop"], attn["banks"], attn["phis"]
            all_before(act, L)

            def exp_relu(name, i):
                k = phis.index(name)
                src = ps[banks.bank[name]]
                act.wait_ge(*L["pe"].done(name, i))
                if k >= NE:
                    act.wait_ge(*L["dve"].done("phi_" + phis[k - NE], i))
                else:
                    last = max(j for j in range(len(phis)) if j % NE == k)
                    act.wait_ge(*L["dve"].done("phi_" + phis[last], i, 1))
                nc.scalar.activation(ee[k % NE][:, :], src[:, :], ACT.Exp).then_inc(*L["act"].step(f"e_{name}"))
                nc.scalar.activation(rr[k % NE][:, :], src[:, :], ACT.Relu).then_inc(*L["act"].step(f"r_{name}"))

            def keys_values(c, i):
                for h in range(2):
                    exp_relu(f"K{c}{h}", i)
                for h in range(2):
                    act.wait_ge(*L["pe"].done(f"V{c}{h}", i))
                    act.wait_ge(*L["pe"].done(f"D{(c - 2) % Q}2", i, 0 if c >= 2 else 1))
                    nc.scalar.copy(vt[c % 2][:, h * H // 2:(h + 1) * H // 2, 0:DH],
                                   ps[banks.bank[f"V{c}{h}"]][:, :].rearrange("p (h d) -> p h d", d=DH))\
                        .then_inc(*L["act"].step(f"v{c}{h}"))

            with act.Fori(0, NT) as i:
                act.wait_ge(*L["pe"].done("nT", i))
                act.wait_ge(*L["pe"].done(f"V{Q - 1}1", i, 1))
                nc.scalar.activation(ahn[:, :], ps[banks.bank["nT"]][:, :], ACT.Identity, scale=affine[:, 0:1],
                                     bias=affine[:, 1:2]).then_inc(*L["act"].step("hf"))
                for p in range(PR):
                    exp_relu(f"Q{p}", i)
                keys_values(0, i)
                for c in C:
                    for j in range(2):
                        act.wait_ge(*L["pe"].done(f"KT{c}{j}", i))
                        act.wait_ge(*L["pe"].done(f"S{(c - 2) % Q}b1", i, 0 if c >= 2 else 1))
                        nc.scalar.copy(kf[c % 2][:, 4 * j:4 * j + 4, :],
                                       ps[banks.bank[f"KT{c}{j}"]][:, :].rearrange("p (k n) -> p k n", n=P))\
                            .then_inc(*L["act"].step(f"kt{c}{j}"))
                    if c + 1 < Q:
                        keys_values(c + 1, i)
                    for j in range(2):
                        act.wait_ge(*L["pe"].done(f"OT{c}{j}", i))
                        act.wait_ge(*L["pe"].done("WO", i, 1))
                        nc.scalar.copy(of[:, 4 * j:4 * j + 4, c * P:(c + 1) * P],
                                       ps[banks.bank[f"OT{c}{j}"]][:, :].rearrange("p (k n) -> p k n", n=P))\
                            .then_inc(*L["act"].step(f"ot{c}{j}"))
                act.wait_ge(*L["pe"].done("WO", i))
                act.wait_ge(*L["pe"].done("yT", i, 1))
                nc.scalar.copy(ayf[:, :], ps[banks.bank["WO"]][:, :]).then_inc(*L["act"].step("wf"))

            ffn_act(ffn2)
            ffn_act(ffn3)

        @block.vector
        def _(dve):
            S = setup["dve"]
            nc.vector.memset(power[:, 0:1], -0.5).then_inc(pe_did, PRIME)
            nc.vector.memset(power[:, 1:2], -0.5).then_inc(act_did, PRIME)
            nc.vector.memset(power[:, 2:3], -0.5).then_inc(pool_did, PRIME)
            nc.vector.memset(power[:, 3:4], -0.5).then_inc(dve_did, PRIME)
            for k, s_ in enumerate((*out_x, out_y, out_xs)):
                nc.vector.memset(spare[:, k + 1:k + 2], 0.0).then_inc(s_, 16)
            nc.vector.memset(s3[:, :], 0.0).then_inc(*S.step("prime"))
            dve.wait_ge(*S.done("prime", 0))
            dve.wait_ge(*setup["pe"].done("vT", 0))
            nc.vector.tensor_copy(sc[:, :], ps[7][:, 0:NV]).then_inc(*S.step("vec"))
            dve.wait_ge(*S.done("vec", 0))
            nc.vector.tensor_scalar(s3[:, :], sc[:, 4 * KT:4 * KT + 1], 0.5, None, ALU.mult).then_inc(*S.step("const"))
            for g, (col, _) in enumerate(groups):
                dve.wait_ge(*setup["pe"].done(f"wT{g}", 0))
                cols = slice(col, col + TILE)
                nc.vector.tensor_copy(wh[:, cols], ps[g % 8][:, :]).then_inc(*S.step(f"hi{g}"))
                dve.wait_ge(*S.done(f"hi{g}", 0))
                nc.vector.tensor_tensor(wl[:, cols], ps[g % 8][:, :], wh[:, cols].bitcast(F32), ALU.subtract)\
                    .then_inc(*S.step(f"lo{g}"))
            dve.wait_ge(in_w, 6 * 16)
            nc.vector.tensor_copy(fh[:, :], sf[:, :]).then_inc(*S.step("fhi"))
            dve.wait_ge(*S.done("fhi", 0))
            nc.vector.tensor_tensor(fl[:, :], sf[:, :], fh[:, :].bitcast(F32), ALU.subtract).then_inc(*S.step("flo"))

            def ffn_dve(f):
                G, L, n = f["pro"], f["loop"], f["n"]
                tern = f["kind"] == "ternary"
                loads = n * (NI + 1)

                def stats(u, U, X, i, arrived):
                    dve.wait_ge(in_ln[u], arrived)
                    for q in range(Q):
                        ins = nc.vector.bn_stats(bst[u][:, q, :], xln[u][:, q, :])
                    ins.then_inc(*X["dve"].step(f"st{U}"))
                    dve.wait_ge(*X["dve"].done(f"st{U}", i))
                    nc.vector.memset(spare[:, 0:1], 0.0)
                    for q in range(Q):
                        ins = nc.vector.bn_aggr(bag[u][:, q, :], bst[u][:, q, :])
                    ins.then_inc(*X["dve"].step(f"ag{U}"))
                    dve.wait_ge(*X["dve"].done(f"ag{U}", i))
                    nc.vector.tensor_scalar(ve[u][:, :], bag[u][:, :, 1], EPS_LN, None, ALU.add)\
                        .then_inc(*X["dve"].step(f"ve{U}"))
                    dve.wait_ge(*X["pool"].done(f"rs{U}", i))
                    if X is L:
                        dve.wait_ge(*X["pe"].done(f"nT{U}", i, 1))
                    for q in range(Q):
                        ins = nc.vector.tensor_scalar(xn[u][:, q, :], xln[u][:, q, :], bag[u][:, q, 0:1],
                                                      rs[u][:, q:q + 1], ALU.subtract, ALU.mult)
                    ins.then_inc(*X["dve"].step(f"xn{U}"))

                def leading(X, name, src, dst, i):
                    nc.vector.tensor_copy(dst, src[:, :]).then_inc(*X["dve"].step(f"hi_{name}"))

                all_before(dve, G)
                for u, U in enumerate(PAIR):
                    stats(u, U, G, 0, 16 * (loads + 1))
                for u, U in enumerate(PAIR):
                    dve.wait_ge(*G["act"].done(f"hf{U}", 0))
                    leading(G, f"n{U}", full[u], nh[u][:, :], 0)
                all_before(dve, L)

                def slot(name):
                    return full[f["splits"].index(name) % NF]

                def slot_free(name, i):
                    k = f["splits"].index(name)
                    if k >= NF:
                        dve.wait_ge(*L["pool"].done("lo_" + f["splits"][k - NF], i))
                    else:
                        last = max(j for j in range(len(f["splits"])) if j % NF == k)
                        dve.wait_ge(*L["pool"].done("lo_" + f["splits"][last], i, 1))

                def norm(u, U, i):
                    dve.wait_ge(*L["act"].done(f"hf{U}", i))
                    dve.wait_ge(*L["pe"].done((f"v{U}{KT - 1}" if tern else f"L1{U}{KT - 1}"), i))
                    leading(L, f"n{U}", slot(f"n{U}"), nh[u][:, :], i)

                def gated(u, U, i):
                    dve.wait_ge(*L["pe"].done(f"W3{U}", i, 1))
                    for m in range(KT):
                        name = f"{U}{m}"
                        k = f["gates"].index(name)
                        dve.wait_ge(*L["pe"].done(f"v{name}", i))
                        dve.wait_ge(*L["act"].done(f"silu{name}", i))
                        slot_free(f"L1{name}", i)
                        nc.vector.scalar_tensor_tensor(slot(f"L1{name}")[:, :], ps[f["banks"].bank[f"v{name}"]][:, :],
                                                       sc[:, KT + m:KT + m + 1], gate[k % NS][:, :], ALU.mult, ALU.mult)\
                            .then_inc(*L["dve"].step(f"mul{name}"))
                        dve.wait_ge(*L["dve"].done(f"mul{name}", i))
                        leading(L, f"L1{name}", slot(f"L1{name}"), ah[u][0][:, m, :], i)

                def activated(name, dst, reader, back, u, U, i):
                    dve.wait_ge(*L["pe"].done(reader, i, back))
                    for m in range(KT):
                        dve.wait_ge(*L["act"].done(f"gelu_{name}{U}{m}", i))
                        leading(L, f"{name}{U}{m}", slot(f"{name}{U}{m}"), ah[u][dst][:, m, :], i)

                with dve.Fori(0, NI) as i:
                    for u, U in enumerate(PAIR):
                        if tern:
                            gated(u, U, i)
                        else:
                            activated("L1", 0, f"W3{U}", 1, u, U, i)
                        stats(u, U, L, i, i * 16 + 16 * (loads + 2))
                    norm(0, "A", i)
                    if tern:
                        activated("H1", 1, f"H2A{KT - 1}", 1, 0, "A", i)
                        norm(1, "B", i)
                        activated("H1", 1, f"H2B{KT - 1}", 1, 1, "B", i)
                        activated("H2", 0, f"H1A{KT - 1}", 0, 0, "A", i)
                        activated("H2", 0, f"H1B{KT - 1}", 0, 1, "B", i)
                    else:
                        norm(1, "B", i)
                    for u, U in enumerate(PAIR):
                        dve.wait_ge(*L["pe"].done(f"yT{U}", i))
                        dve.wait_ge(in_res[u], i * 16 + 16 * (n * NI + 1))
                        dve.wait_ge(out_x[u], i * 16 + 16 * (n * NI + 1))
                        nc.vector.tensor_tensor(xo[u][:, :, :], ps[f["banks"].bank[f"yT{U}"]][:, :].rearrange("p (q d) -> p q d", d=D),
                                                xres[u][:, :, :], ALU.add).then_inc(*L["dve"].step(f"res{U}"))

            ffn_dve(ffn1)

            L, banks, phis = attn["loop"], attn["banks"], attn["phis"]
            V = L["dve"]
            all_before(dve, L)
            for k in range(2):
                nc.vector.memset(vt[k][:, :, DH:DH + 1], 1.0)
                nc.vector.memset(vt[k][:, :, DH + 1:DH + 2], 0.0)

            def phi(name, dst, i):
                k = phis.index(name)
                dve.wait_ge(*L["act"].done(f"r_{name}", i))
                nc.vector.scalar_tensor_tensor(dst, ee[k % NE][:, :], 1.0, rr[k % NE][:, :], ALU.min, ALU.add)\
                    .then_inc(*V.step(f"phi_{name}"))

            def keys(c, i):
                dve.wait_ge(*L["pe"].done(f"D{(c - 2) % Q}2", i, 0 if c >= 2 else 1))
                for h in range(2):
                    phi(f"K{c}{h}", kt_[c % 2][:, h * TILE:(h + 1) * TILE], i)

            def small(name, i, ins):
                ins.then_inc(*V.step(name))
                dve.wait_ge(*V.done(name, i))

            with dve.Fori(0, NB) as b_:
                nc.vector.memset(state[:, :, :], 0.0)
                with dve.Fori(0, SUP) as s_:
                    i = b_ * SUP + s_
                    dve.wait_ge(in_ax, i * 16 + 16)
                    for q in range(Q):
                        ins = nc.vector.bn_stats(abst[:, q, :], ax[:, q, :])
                    small("st", i, ins)
                    nc.vector.memset(spare[:, 0:1], 0.0)
                    for q in range(Q):
                        ins = nc.vector.bn_aggr(abag[:, q, :], abst[:, q, :])
                    small("ag", i, ins)
                    small("ve", i, nc.vector.tensor_scalar(av[:, :], abag[:, :, 1], EPS_LN, None, ALU.add))
                    dve.wait_ge(*L["pool"].done("r1", i))
                    small("v1", i, nc.vector.tensor_tensor(av1[:, :], abag[:, :, 1], ar1[:, :], ALU.mult))
                    small("v2", i, nc.vector.tensor_tensor(av2[:, :], av1[:, :], ar1[:, :], ALU.mult))
                    nc.vector.tensor_scalar(av3[:, :], av2[:, :], EPS_LN, None, ALU.add).then_inc(*V.step("v3"))
                    for q in range(Q):
                        ins = nc.vector.tensor_scalar(axp[:, q, :], ax[:, q, :], abag[:, q, 0:1], ar1[:, q:q + 1],
                                                      ALU.subtract, ALU.mult)
                    small("xp", i, ins)
                    dve.wait_ge(*L["pool"].done("r2", i))
                    for q in range(Q):
                        ins = nc.vector.tensor_scalar(axn[:, q, :], axp[:, q, :], ar2[:, q:q + 1], None, ALU.mult)
                    ins.then_inc(*V.step("xn"))
                    for p in range(PR):
                        phi(f"Q{p}", qf[:, p, :], i)
                    keys(0, i)
                    for c in C:
                        k = c % 2
                        for n, g in enumerate(SG):
                            dve.wait_ge(*L["pe"].done(f"S{c}{g}", i))
                            dve.wait_ge(*L["pe"].done(f"O{(c - 2) % Q}2", i, 0 if c >= 2 else 1))
                            nc.vector.tensor_tensor(am[k][:, n, :, :], ps[banks.bank[f"S{c}{g}"]][:, :].rearrange("p (h n) -> p h n", n=P),
                                                    mask[:, :, :], ALU.mult).then_inc(*V.step(f"am{c}{g}"))
                        if c + 1 < Q:
                            keys(c + 1, i)
                        dve.wait_ge(*L["pe"].done(f"OT{(c - 2) % Q}1", i, 0 if c >= 2 else 1))
                        for g, (p0, p1) in enumerate(OG):
                            nh_ = 2 * (p1 - p0)
                            src = ps[banks.bank[f"O{c}{g}"]][:, 0:nh_ * HW].rearrange("p (h w) -> p h w", w=HW)
                            dve.wait_ge(*L["pe"].done(f"O{c}{g}", i))
                            small(f"dm{c}{g}", i, nc.vector.tensor_scalar(den[g % 2][:, 0:nh_], src[:, :, DH], EPS_DEN, None, ALU.max))
                            small(f"rd{c}{g}", i, nc.vector.reciprocal(rden[g % 2][:, 0:nh_], den[g % 2][:, 0:nh_]))
                            nc.vector.tensor_tensor(ot[k][:, 2 * p0:2 * p1, :], src[:, :, 0:DH],
                                                    rden[g % 2][:, 0:nh_].unsqueeze(2).to_broadcast([P, nh_, DH]), ALU.mult)\
                                .then_inc(*V.step(f"on{c}{g}"))
                        for g, (p0, p1) in enumerate(OG):
                            src = ps[banks.bank[f"D{c}{g}"]][:, 0:(p1 - p0) * PW].rearrange("p (k w) -> p k w", w=PW)
                            dve.wait_ge(*L["pe"].done(f"D{c}{g}", i))
                            for name, rows, cols in (("sa", slice(0, DH), slice(0, HW)), ("sb", slice(DH, P), slice(HW, PW))):
                                nc.vector.tensor_tensor(state[rows, p0:p1, cols], src[rows, :, cols], state[rows, p0:p1, cols],
                                                        ALU.add).then_inc(*V.step(f"{name}{c}{g}"))
                    dve.wait_ge(*L["pe"].done("yT", i))
                    dve.wait_ge(out_y, i * 16 + 16)
                    dve.wait_ge(out_xs, i * 16 + 16)
                    small("y", i, nc.vector.tensor_tensor(ay[:, :, :], ps[banks.bank["yT"]][:, :].rearrange("p (q d) -> p q d", d=D),
                                                          axp[:, :, :], ALU.add))
                    nc.vector.tensor_tensor(axs[:, :, :], ay[:, :, :], ax[:, :, :], ALU.add).then_inc(*V.step("ys"))

            ffn_dve(ffn2)
            ffn_dve(ffn3)

        @block.gpsimd
        def _(pool):
            S = setup["pool"]
            pool.wait_ge(pool_did, PRIME)
            nc.gpsimd.memset(ident[:, :], 0.0).then_inc(*S.step("ones"))
            pool.wait_ge(*S.done("ones", 0))
            nc.gpsimd.affine_select(out=ident[:, :], in_=ident[:, :], compare_op=ALU.not_equal, fill=1.0, base=0,
                                    pattern=[[-1, P]], channel_multiplier=1).then_inc(*S.step("ident"))
            nc.gpsimd.memset(mask[:, :, :], 1.0).then_inc(*S.step("mask1"))
            pool.wait_ge(*S.done("mask1", 0))
            nc.gpsimd.affine_select(out=mask[:, :, :], in_=mask[:, :, :], compare_op=ALU.is_ge, fill=0.0, base=0,
                                    pattern=[[0, 4], [1, P]], channel_multiplier=-1).then_inc(*S.step("mask"))

            def ffn_pool(f):
                G, L = f["pro"], f["loop"]
                tern = f["kind"] == "ternary"

                def rest(X, name, src, hi, dst, i):
                    pool.wait_ge(*X["dve"].done(f"hi_{name}", i))
                    nc.gpsimd.tensor_tensor(dst, src[:, :], hi.bitcast(F32), ALU.subtract)\
                        .then_inc(*X["pool"].step(f"lo_{name}"))

                def rstd(u, U, X, i):
                    pool.wait_ge(*X["dve"].done(f"ve{U}", i))
                    nc.gpsimd.tensor_tensor(rs[u][:, :], ve[u][:, :], power[:, :], ALU.pow).then_inc(*X["pool"].step(f"rs{U}"))

                all_before(pool, G)
                for u, U in enumerate(PAIR):
                    rstd(u, U, G, 0)
                for u, U in enumerate(PAIR):
                    rest(G, f"n{U}", full[u], nh[u][:, :], nl[u][:, :], 0)
                all_before(pool, L)

                def slot(name):
                    return full[f["splits"].index(name) % NF]

                def layer(name, dst, u, U, i):
                    for m in range(KT):
                        rest(L, f"{name}{U}{m}", slot(f"{name}{U}{m}"), ah[u][dst][:, m, :], al[u][dst][:, m, :], i)

                def norm(u, U, i):
                    rest(L, f"n{U}", slot(f"n{U}"), nh[u][:, :], nl[u][:, :], i)

                with pool.Fori(0, NI) as i:
                    for u, U in enumerate(PAIR):
                        layer("L1", 0, u, U, i)
                        rstd(u, U, L, i)
                    norm(0, "A", i)
                    if tern:
                        layer("H1", 1, 0, "A", i)
                        norm(1, "B", i)
                        layer("H1", 1, 1, "B", i)
                        layer("H2", 0, 0, "A", i)
                        layer("H2", 0, 1, "B", i)
                    else:
                        norm(1, "B", i)

            ffn_pool(ffn1)

            L = attn["loop"]
            all_before(pool, L)
            with pool.Fori(0, NT) as i:
                pool.wait_ge(*L["dve"].done("ve", i))
                nc.gpsimd.tensor_tensor(ar1[:, :], av[:, :], power[:, :], ALU.pow).then_inc(*L["pool"].step("r1"))
                pool.wait_ge(*L["dve"].done("v3", i))
                nc.gpsimd.tensor_tensor(ar2[:, :], av3[:, :], power[:, :], ALU.pow).then_inc(*L["pool"].step("r2"))

            ffn_pool(ffn2)
            ffn_pool(ffn3)


_INS = ["L0_attn_x", "L0_attn_ln1_g", "L0_attn_ln1_b", "L0_attn_Wq", "L0_attn_Wk", "L0_attn_Wv", "L0_attn_Wo",
        "L0_attn_ln2_g", "L0_attn_ln2_b", "L0_attn_Wf1", "L0_attn_Wf2", "L0_ffn_w1_w", "L0_ffn_w1_s", "L0_ffn_w2_w",
        "L0_ffn_w2_s", "L0_ffn_h1_w", "L0_ffn_h1_s", "L0_ffn_h2_w", "L0_ffn_h2_s", "L0_ffn_w3_w", "L0_ffn_w3_s"]


def kernel(**inputs):
    import numpy as np
    import concourse.bacc as bacc
    from concourse.bass_utils import run_bass_kernel_spmd

    nc = bacc.Bacc("TRN2", target_bir_lowering=False, num_devices=1)
    arrays, args = {}, {}
    for name in _INS:
        a = np.ascontiguousarray(inputs[name])
        arrays[f"in_{name}"] = a
        args[name] = nc.dram_tensor(f"in_{name}", a.shape, mybir.dt.from_np(a.dtype), kind="ExternalInput").ap()
    x = arrays["in_L0_attn_x"]
    out = nc.dram_tensor("out_0", x.shape, mybir.dt.from_np(x.dtype), kind="ExternalOutput").ap()
    build_kernel(nc, args, out.rearrange("b t d -> (b t) d"))
    got = run_bass_kernel_spmd(nc, [arrays], core_ids=[0])
    return got.results[0]["out_0"]
```

```python
from contextlib import ExitStack

import concourse.bass as bass
from concourse import mybir

P = 128
ALU = mybir.AluOpType
ACT = mybir.ActivationFunctionType
F32 = mybir.dt.float32
F32R = mybir.dt.float32r
EPS_LN = 1e-5
EPS_DEN = 1e-6

TILE = 512
Q = TILE // P
PAIR = ("A", "B")


class Steps:

    def __init__(self, sem, base, names):
        assert len(set(names)) == len(names)
        self.sem, self.base, self.names = sem, base, names
        self.at = {name: n + 1 for n, name in enumerate(names)}
        self.next = 0

    def step(self, name):
        assert self.names[self.next % len(self.names)] == name, (name, self.names[self.next % len(self.names)])
        self.next += 1
        return self.sem, 1

    def done(self, name, i, back=0):
        return self.sem, i * len(self.names) + (self.base + self.at[name] - back * len(self.names))

    def end(self, iterations):
        return self.base + iterations * len(self.names)


class Ring:

    def __init__(self, jobs, size, loop=True):
        self.place, self.before = {}, {}
        for n, job in enumerate(jobs):
            self.place[job] = n % size
            if n >= size:
                self.before[job] = (jobs[n - size], 0)
            elif loop:
                self.before[job] = (jobs[max(j for j in range(len(jobs)) if j % size == n)], 1)
            else:
                self.before[job] = None

    def prior(self, job):
        return self.before[job]


class Banks:

    def __init__(self, jobs, loop=True):
        self.bank = {job: bank for job, bank, _, _ in jobs}
        self.prior = {}
        for n, (job, bank, _, _) in enumerate(jobs):
            same = [k for k, j in enumerate(jobs) if j[1] == bank]
            before = [k for k in same if k < n]
            if before or loop:
                k = before[-1] if before else same[-1]
                self.prior[job] = (jobs[k][2], jobs[k][3], 0 if before else 1)

    def wait_empty(self, eng, job, i):
        if job in self.prior:
            steps, name, back = self.prior[job]
            eng.wait_ge(*steps.done(name, i, back))


def build_kernel(nc, t, out):
    x_in = t["L0_attn_x"].rearrange("b t d -> (b t) d")
    NTOK, D = x_in.shape
    DH_ = t["L0_ffn_h1_w"].shape[0]
    KT = DH_ // P
    DA = t["L0_attn_Wq"].shape[1]
    DH = 64
    H = DA // DH
    PR = H // 2
    NB = t["L0_attn_x"].shape[0]
    NT = NTOK // TILE
    NI = NT // 2
    SUP = NT // NB
    HW = DH + 2
    PW = 2 * HW
    OG = [(0, 3), (3, 6), (6, 8)]
    assert D == P and NTOK % (2 * TILE) == 0 and H == 16 and KT == 4 and t["L0_attn_Wf1"].shape[1] == DH_

    W1, W2, H1, H2, W3 = 0, DH_, 2 * DH_, 2 * DH_ + KT * DH_, 2 * DH_ + 2 * KT * DH_
    WCOLS = W3 + DH_

    ctx = ExitStack()

    def sem(name):
        return ctx.enter_context(nc.semaphore(name))

    def sb(stack, name, shape, dt=F32):
        return stack.enter_context(nc.sbuf_tensor(name, shape, dt))

    def view(dram):
        return dram.rearrange("(n q p) d -> n p q d", q=Q, p=P)

    with ctx:
        ident = sb(ctx, "ident", [P, P])
        mask = sb(ctx, "mask", [P, 4, P])
        wh = sb(ctx, "wh", [P, WCOLS], F32R)
        wl = sb(ctx, "wl", [P, WCOLS], F32R)
        fh = sb(ctx, "fh", [P, 2 * DH_], F32R)
        fl = sb(ctx, "fl", [P, 2 * DH_], F32R)
        wah = sb(ctx, "wah", [P, 4 * DA], F32R)
        wal = sb(ctx, "wal", [P, 4 * DA], F32R)
        NV = 4 * KT + 5
        sc = sb(ctx, "sc", [P, NV])
        s3 = sb(ctx, "s3", [P, 1])
        affine = sc[:, NV - 4:NV]
        spare = sb(ctx, "spare", [P, 5])
        power = sb(ctx, "power", [P, Q])
        x1_d = nc.dram_tensor("x1_scratch", (NTOK, D), F32).ap()
        y_d = nc.dram_tensor("y_scratch", (NTOK, D), F32).ap()
        xs_d = nc.dram_tensor("xs_scratch", (NTOK, D), F32).ap()
        x2_d = nc.dram_tensor("x2_scratch", (NTOK, D), F32).ap()
        ps = [ctx.enter_context(nc.psum_tensor(f"ps{b}", [P, TILE], F32)) for b in range(8)]

        with ExitStack() as s:
            st1 = sb(s, "st1", [P, KT, D])
            st2 = sb(s, "st2", [P, KT, D])
            sh1 = sb(s, "sh1", [P, KT, DH_])
            sh2 = sb(s, "sh2", [P, KT, DH_])
            st3 = sb(s, "st3", [P, DH_])
            sf = sb(s, "sf", [P, 2 * DH_])
            sa = sb(s, "sa", [P, 4 * DA])
            vec = sb(s, "vec", [NV, P])

        with ExitStack() as s:
            xln = [sb(s, f"xln{u}", [P, Q, D]) for u in PAIR]
            xres = [sb(s, f"xres{u}", [P, Q, D]) for u in PAIR]
            xn = [sb(s, f"xn{u}", [P, Q, D]) for u in PAIR]
            nh = [sb(s, f"nh{u}", [P, TILE], F32R) for u in PAIR]
            nl = [sb(s, f"nl{u}", [P, TILE], F32R) for u in PAIR]
            ah = [[sb(s, f"ah{u}{k}", [P, KT, TILE], F32R) for k in range(2)] for u in PAIR]
            al = [[sb(s, f"al{u}{k}", [P, KT, TILE], F32R) for k in range(2)] for u in PAIR]
            NF = 6
            full = [sb(s, f"full{k}", [P, TILE]) for k in range(NF)]
            NS = 3
            gate = [sb(s, f"gate{k}", [P, TILE]) for k in range(NS)]
            yf = [sb(s, f"yf{u}", [P, TILE]) for u in PAIR]
            xo = [sb(s, f"xo{u}", [P, Q, D]) for u in PAIR]
            bst = [sb(s, f"bst{u}", [P, Q, 6]) for u in PAIR]
            bag = [sb(s, f"bag{u}", [P, Q, 2]) for u in PAIR]
            ve = [sb(s, f"ve{u}", [P, Q]) for u in PAIR]
            rs = [sb(s, f"rs{u}", [P, Q]) for u in PAIR]

        with ExitStack() as s:
            ax = sb(s, "ax", [P, Q, D])
            axr = sb(s, "axr", [P, Q, D])
            axp = sb(s, "axp", [P, Q, D])
            axc = sb(s, "axc", [P, Q, D])
            axn = sb(s, "axn", [P, Q, D])
            ahh = [sb(s, f"ahh{h}", [P, TILE // 2], F32R) for h in range(2)]
            ahl = [sb(s, f"ahl{h}", [P, TILE // 2], F32R) for h in range(2)]
            ahf = sb(s, "ahf", [P, TILE // 2])
            qf = [sb(s, f"qf{h}", [P, PR, TILE // 2]) for h in range(2)]
            kt_ = [sb(s, f"kt{k}", [P, DA]) for k in range(2)]
            vt = [sb(s, f"vt{k}", [P, H, HW]) for k in range(2)]
            kf = sb(s, "kf", [P, PR, P])
            am = sb(s, "am", [P, 4, 4, P])
            state = sb(s, "state", [P, PR, PW])
            ot = sb(s, "ot", [P, H, DH])
            oh = sb(s, "oh", [P, PR, TILE // 2], F32R)
            ol = sb(s, "ol", [P, PR, TILE // 2], F32R)
            NE = 2
            ee = [sb(s, f"ee{k}", [P, TILE]) for k in range(NE)]
            rr = [sb(s, f"rr{k}", [P, TILE]) for k in range(NE)]
            den = sb(s, "den", [P, 3, 6])
            rden = sb(s, "rden", [P, 3, 6])
            ayf = sb(s, "ayf", [P, TILE])
            ay = sb(s, "ay", [P, Q, D])
            axs = sb(s, "axs", [P, Q, D])
            abst = sb(s, "abst", [P, Q, 6])
            abag = sb(s, "abag", [P, Q, 2])
            av, ar1, av1, av2, av3, ar2 = (sb(s, f"as{k}", [P, Q]) for k in range(6))

        pe_did, act_did, dve_did, pool_did = sem("pe_did"), sem("act_did"), sem("dve_did"), sem("pool_did")
        in_w, in_wt, in_v = sem("in_w"), sem("in_wt"), sem("in_v")
        in_ln = [sem(f"in_ln{u}") for u in PAIR]
        in_res = [sem(f"in_res{u}") for u in PAIR]
        out_x = [sem(f"out_x{u}") for u in PAIR]
        in_ar = sem("in_ar")
        in_ax, out_y, out_xs = sem("in_ax"), sem("out_y"), sem("out_xs")

        PRIME = 512
        ENG = ("pe", "act", "dve", "pool")
        sems = dict(pe=pe_did, act=act_did, dve=dve_did, pool=pool_did)
        base = dict.fromkeys(ENG, PRIME)
        plan = []

        def phase(iterations, **names):
            steps = {e: Steps(sems[e], base[e], names.get(e, [])) for e in ENG}
            for e in ENG:
                base[e] = steps[e].end(iterations)
            plan.append(steps)
            return steps

        def all_before(eng, steps):
            for e in ENG:
                eng.wait_ge(steps[e].sem, steps[e].base)

        groups = ([(W1, [st1[:, m, :] for m in range(KT)])] + [(W2, [st2[:, m, :] for m in range(KT)])]
                  + [(H1 + k * DH_, [sh1[:, m, k * P:(k + 1) * P] for m in range(KT)]) for k in range(KT)]
                  + [(H2 + k * DH_, [sh2[:, m, k * P:(k + 1) * P] for m in range(KT)]) for k in range(KT)]
                  + [(W3, [st3[:, k * P:(k + 1) * P] for k in range(KT)])])
        NG = len(groups)
        setup = phase(1, pe=["vT"] + [f"wT{g}" for g in range(NG)],
                      dve=["prime", "vec", "const"] + [f"{w}{g}" for g in range(NG) for w in ("hi", "lo")]
                      + ["fhi", "flo", "ahi", "alo"],
                      pool=["ones", "ident", "mask1", "mask"])

        LAYERS = {"ternary": ["L1", "H1", "H2", "W3"], "plain": ["L1", "W3"]}

        def ffn_plan(kind):
            tern = kind == "ternary"
            pe, act, dve, pool, splits, gates = [], [], [], [], [], []

            def split(name):
                splits.append(name)
                dve.append(f"hi_{name}")
                pool.append(f"lo_{name}")

            def layer(name, u):
                for m in range(KT):
                    if name == "L1" and tern:
                        pe.extend([f"g{u}{m}", f"v{u}{m}"])
                        act.append(f"silu{u}{m}")
                        gates.append(f"{u}{m}")
                        dve.append(f"mul{u}{m}")
                    else:
                        pe.append(f"{name}{u}{m}")
                        act.append(f"gelu_{name}{u}{m}")
                    split(f"{name}{u}{m}")

            def stats(u):
                dve.extend([f"st{u}", f"ag{u}", f"ve{u}", f"xn{u}"])
                pool.append(f"rs{u}")

            def norm(u):
                pe.append(f"nT{u}")
                act.append(f"hf{u}")
                split(f"n{u}")

            seq = LAYERS[kind]
            layer(seq[0], "A")
            stats("A")
            layer(seq[0], "B")
            stats("B")
            norm("A")
            for k, name in enumerate(seq[1:-1]):
                layer(name, "A")
                if k == 0:
                    norm("B")
                layer(name, "B")
            pe.append("W3A")
            act.append("yA")
            if not tern:
                norm("B")
            pe.extend(["W3B", "yTA", "yTB"])
            act.append("yB")
            dve.extend(["resA", "resB"])
            pro_dve = [f"{n}{u}" for u in PAIR for n in ("st", "ag", "ve", "xn")] + [f"hi_n{u}" for u in PAIR]
            pro_pool = [f"rs{u}" for u in PAIR] + [f"lo_n{u}" for u in PAIR]
            pro = phase(1, pe=["nTA", "nTB"], act=["hfA", "hfB"], dve=pro_dve, pool=pro_pool)
            loop = phase(NI, pe=pe, act=act, dve=dve, pool=pool)
            A, V = loop["act"], loop["dve"]
            jobs, n = [], 0
            for name in pe:
                if name[:2] == "nT":
                    jobs.append((name, 6, A, "hf" + name[2]))
                elif name[:2] == "yT":
                    jobs.append((name, 7, V, "res" + name[2]))
                else:
                    if name[:2] == "W3":
                        by = (A, "y" + name[2])
                    elif name[0] == "g":
                        by = (A, "silu" + name[1:])
                    elif name[0] == "v":
                        by = (V, "mul" + name[1:])
                    else:
                        by = (A, "gelu_" + name)
                    jobs.append((name, n % 6, *by))
                    n += 1
            return dict(kind=kind, pro=pro, loop=loop, banks=Banks(jobs), splits=splits, gates=gates)

        ffn1 = ffn_plan("ternary")

        C = range(Q)
        SG = ("a0", "b0", "a1", "b1")

        def attention_plan():
            lists = {}
            for part in ("pro", "loop"):
                pe, act, dve, pool, phis, jobs, count = [], [], [], [], [], [], {"P": 0, "O": 0}

                def job(ring, name, eng, by):
                    pe.append(name)
                    jobs.append((name, count[ring] % 2 + (0 if ring == "P" else 6), eng, by))
                    count[ring] += 1

                def phi(name):
                    phis.append(name)
                    job("P", name, "act", f"r_{name}")
                    act.extend([f"e_{name}", f"r_{name}"])
                    dve.append(f"phi_{name}")

                def kv(c):
                    for h in range(2):
                        phi(f"K{c}{h}")
                    for h in range(2):
                        job("P", f"V{c}{h}", "act", f"v{c}{h}")
                        act.append(f"v{c}{h}")

                def norm(h):
                    job("P", f"nT{h}", "act", f"hf{h}")
                    act.append(f"hf{h}")
                    dve.extend([f"hh{h}", f"hl{h}"])

                def kt(c):
                    for j in range(2):
                        job("P", f"KT{c}{j}", "act", f"kf{c}{j}")
                        act.append(f"kf{c}{j}")

                def scores(c, j):
                    for g in ("a", "b"):
                        pe.append(f"S{c}{g}{j}")
                        jobs.append((f"S{c}{g}{j}", 2 + 2 * j + (g == "b"), "dve", f"am{c}{g}{j}"))
                        dve.append(f"am{c}{g}{j}")

                if part == "pro":
                    dve.extend(["st", "ag", "ve", "v1", "v2", "v3", "xp", "xn"])
                    pool.extend(["r1", "r2"])
                    norm(0)
                    norm(1)
                    for j in range(4):
                        phi(f"Q0{j}")
                    kv(0)
                    kt(0)
                    scores(0, 0)
                    scores(0, 1)
                else:
                    for c in C:
                        n = (c + 1) % Q
                        qs = QJOBS[c]
                        kv(n)
                        if c == 0:
                            act.append("cp")
                        for g in range(3):
                            job("O", f"O{c}{g}", "dve", f"on{c}{g}")
                            dve.extend([f"dm{c}{g}", f"rd{c}{g}", f"on{c}{g}"])
                            if g < len(qs):
                                phi(f"Q{qs[g]}")
                        if c == 0:
                            dve.extend(["st", "ag", "ve"])
                            pool.append("r1")
                        if c in (1, 3):
                            norm(c // 2)
                        kt(n)
                        for g in range(3):
                            job("O", f"D{c}{g}", "dve", f"sb{c}{g}")
                            dve.extend([f"sa{c}{g}", f"sb{c}{g}"])
                        if c == 0:
                            dve.extend(["v1", "v2", "v3", "xp"])
                            pool.append("r2")
                        for j in range(2):
                            job("P", f"OT{c}{j}", "dve", f"ol{c}{j}")
                            act.append(f"oh{c}{j}")
                            dve.append(f"ol{c}{j}")
                        if c % 2:
                            scores(n, 0)
                            job("P", f"WO{c // 2}", "act", f"wf{c // 2}")
                            act.append(f"wf{c // 2}")
                            scores(n, 1)
                        else:
                            scores(n, 0)
                            scores(n, 1)
                        if c == 0:
                            dve.append("xn")
                    job("P", "yT", "dve", "y")
                    dve.append("y")
                    pool.append("ys")
                lists[part] = (pe, act, dve, pool, phis, jobs)
            made = {}
            for part, its in (("pro", 1), ("loop", NT)):
                pe, act, dve, pool, phis, jobs = lists[part]
                X = phase(its, pe=pe, act=act, dve=dve, pool=pool)
                X["loop"] = part == "loop"
                X["phis"] = Ring(phis, NE, part == "loop")
                X["banks"] = Banks([(j, b, X[e], by) for j, b, e, by in jobs], part == "loop")
                made[part] = X
            return made

        QJOBS = (("10", "11"), ("12", "13"), ("00", "01"), ("02", "03"))
        attn = attention_plan()
        ffn2 = ffn_plan("plain")
        ffn3 = ffn_plan("ternary")
        ffn1.update(n=0, ln=x_in, res=x_in, dst=x1_d, hi=wh, lo=wl, gain=None)
        ffn2.update(n=1, ln=y_d, res=xs_d, dst=x2_d, hi=fh, lo=fl, gain=(affine[:, 2:3], affine[:, 3:4]))
        ffn3.update(n=2, ln=x2_d, res=x2_d, dst=out, hi=wh, lo=wl, gain=None)

        block = ctx.enter_context(nc.Block())

        @block.sync
        def _(sp):
            for dst, name in ((st1, "w1"), (st2, "w2"), (sh1, "h1"), (sh2, "h2")):
                sp.dma_start(dst[:, :, :], t[f"L0_ffn_{name}_w"].rearrange("(m p) i -> p m i", p=P)).then_inc(in_wt, 16)
            sp.dma_start(st3[:, :], t["L0_ffn_w3_w"]).then_inc(in_wt, 16)
            sp.dma_start(sf[:, 0:DH_], t["L0_attn_Wf1"]).then_inc(in_w, 16)
            sp.dma_start(sf[:, DH_:2 * DH_].rearrange("p (k n) -> p k n", k=KT),
                         t["L0_attn_Wf2"].rearrange("(k p) n -> p k n", p=P)).then_inc(in_w, 16)
            for k, name in enumerate(("w1", "w2", "h1", "h2")):
                sp.dma_start(vec[k * KT:(k + 1) * KT, :],
                             t[f"L0_ffn_{name}_s"].rearrange("(m p) -> m p", p=P)).then_inc(in_v, 16)
            sp.dma_start(vec[4 * KT:4 * KT + 1, :], t["L0_ffn_w3_s"].rearrange("(a p) -> a p", a=1)).then_inc(in_v, 16)
            for k, name in enumerate(("ln1_g", "ln1_b", "ln2_g", "ln2_b")):
                sp.dma_start(vec[4 * KT + 1 + k:4 * KT + 2 + k, :],
                             t[f"L0_attn_{name}"].rearrange("(a p) -> a p", a=1)).then_inc(in_v, 16)
            for k, name in enumerate(("Wq", "Wk", "Wv")):
                sp.dma_start(sa[:, k * DA:(k + 1) * DA], t[f"L0_attn_{name}"]).then_inc(in_w, 16)
            sp.dma_start(sa[:, 3 * DA:4 * DA].rearrange("p (k n) -> p k n", k=PR), t["L0_attn_Wo"].rearrange("(k p) n -> p k n", p=P)).then_inc(in_w, 16)

            def ffn_dma(f):
                n, V, PV = f["n"], f["loop"]["dve"], f["pro"]["dve"]
                src, res, dst = view(f["ln"]), view(f["res"]), view(f["dst"])
                all_before(sp, f["pro"])
                for u in range(2):
                    sp.dma_start(xln[u][:, :, :], src[u]).then_inc(in_ln[u], 16)
                all_before(sp, f["loop"])
                with sp.Fori(0, NI) as i:
                    for u, U in enumerate(PAIR):
                        sp.wait_ge(*V.done(f"xn{U}", i, 1))
                        sp.dma_start(xln[u][:, :, :], src[((i + 1) % NI) * 2 + u]).then_inc(in_ln[u], 16)
                        sp.wait_ge(*V.done(f"res{U}", i, 1))
                        sp.dma_start(xres[u][:, :, :], res[i * 2 + u]).then_inc(in_res[u], 16)
                    for u, U in enumerate(PAIR):
                        sp.wait_ge(*V.done(f"res{U}", i))
                        sp.dma_start(dst[i * 2 + u], xo[u][:, :, :]).then_inc(out_x[u], 16)
                for u in range(2):
                    sp.wait_ge(out_x[u], 16 * NI * (n + 1) + 16)

            ffn_dma(ffn1)

            all_before(sp, attn["pro"])
            sp.dma_start(ax[:, :, :], view(x1_d)[0]).then_inc(in_ax, 16)
            L = attn["loop"]
            all_before(sp, L)
            with sp.Fori(0, NT) as i:
                sp.wait_ge(*L["dve"].done("xp", i, 1))
                sp.dma_start(ax[:, :, :], view(x1_d)[(i + 1) % NT]).then_inc(in_ax, 16)
                sp.wait_ge(*L["pool"].done("ys", i, 1))
                sp.dma_start(axr[:, :, :], view(x1_d)[i]).then_inc(in_ar, 16)
                sp.wait_ge(*L["dve"].done("y", i))
                sp.dma_start(view(y_d)[i], ay[:, :, :]).then_inc(out_y, 16)
                sp.wait_ge(*L["pool"].done("ys", i))
                sp.dma_start(view(xs_d)[i], axs[:, :, :]).then_inc(out_xs, 16)
            sp.wait_ge(out_y, 16 * NT + 16)
            sp.wait_ge(out_xs, 16 * NT + 16)

            ffn_dma(ffn2)
            ffn_dma(ffn3)

        @block.tensor
        def _(pe):
            def transposes(dst, sources, steps, name):
                for k, src in enumerate(sources):
                    ins = nc.tensor.transpose(dst[:, k * P:(k + 1) * P], src, ident[:, :])
                ins.then_inc(*steps.step(name))

            S = setup
            pe.wait_ge(*S["pool"].done("ident", 0))
            pe.wait_ge(in_v, 9 * 16)
            nc.tensor.transpose(ps[7][:, 0:NV], vec[:, :], ident[0:NV, 0:NV]).then_inc(*S["pe"].step("vT"))
            pe.wait_ge(in_wt, 5 * 16)
            for g, (_, sources) in enumerate(groups):
                if g == 7:
                    pe.wait_ge(*S["dve"].done("vec", 0))
                if g >= 8:
                    pe.wait_ge(*S["dve"].done(f"lo{g - 8}", 0))
                transposes(ps[g % 8], sources, S["pe"], f"wT{g}")

            def ffn_pe(f):
                kind, banks, L = f["kind"], f["banks"], f["loop"]
                G = f["pro"]
                all_before(pe, G)
                for u, U in enumerate(PAIR):
                    pe.wait_ge(*G["dve"].done(f"xn{U}", 0))
                    transposes(ps[u], [xn[u][:, q, :] for q in range(Q)], G["pe"], f"nT{U}")
                all_before(pe, L)

                def product(name, i, col, hi_in, lo_in, ks):
                    banks.wait_empty(pe, name, i)
                    b = ps[banks.bank[name]]
                    parts = [(k, xp_, w) for k in ks for xp_, w in ((hi_in, f["hi"]), (lo_in, f["hi"]), (hi_in, f["lo"]))]
                    for n, (k, x_, w) in enumerate(parts):
                        ins = nc.tensor.matmul(b[:, :], w[:, col(k):col(k) + P], x_[:, k, :],
                                               start=(n == 0), stop=(n == len(parts) - 1))
                    ins.then_inc(*L["pe"].step(name))

                def norm(u, U, i):
                    pe.wait_ge(*L["dve"].done(f"xn{U}", i))
                    banks.wait_empty(pe, f"nT{U}", i)
                    transposes(ps[banks.bank[f"nT{U}"]], [xn[u][:, q, :] for q in range(Q)], L["pe"], f"nT{U}")

                def first(u, U, i):
                    hi_in, lo_in = (a[u][:, :].rearrange("p (k n) -> p k n", k=1) for a in (nh, nl))
                    pe.wait_ge(*L["pool"].done(f"lo_n{U}", i, 1))
                    for m in range(KT):
                        if kind == "ternary":
                            product(f"g{U}{m}", i, lambda k: W1 + m * P, hi_in, lo_in, [0])
                            product(f"v{U}{m}", i, lambda k: W2 + m * P, hi_in, lo_in, [0])
                        else:
                            product(f"L1{U}{m}", i, lambda k: m * P, hi_in, lo_in, [0])

                def hidden(name, before, off, src, u, U, i):
                    pe.wait_ge(*L["pool"].done(f"lo_{before}{U}{KT - 1}", i))
                    for m in range(KT):
                        product(f"{name}{U}{m}", i, lambda k: off + k * DH_ + m * P, ah[u][src], al[u][src], range(KT))

                def last(before, off, src, u, U, i):
                    pe.wait_ge(*L["pool"].done(f"lo_{before}{U}{KT - 1}", i))
                    product(f"W3{U}", i, lambda k: off + k * P, ah[u][src], al[u][src], range(KT))

                with pe.Fori(0, NI) as i:
                    first(0, "A", i)
                    first(1, "B", i)
                    norm(0, "A", i)
                    if kind == "ternary":
                        hidden("H1", "L1", H1, 0, 0, "A", i)
                        norm(1, "B", i)
                        hidden("H1", "L1", H1, 0, 1, "B", i)
                        hidden("H2", "H1", H2, 1, 0, "A", i)
                        hidden("H2", "H1", H2, 1, 1, "B", i)
                        last("H2", W3, 0, 0, "A", i)
                        last("H2", W3, 0, 1, "B", i)
                    else:
                        last("L1", DH_, 0, 0, "A", i)
                        norm(1, "B", i)
                        last("L1", DH_, 0, 1, "B", i)
                    for u, U in enumerate(PAIR):
                        pe.wait_ge(*L["act"].done(f"y{U}", i))
                        banks.wait_empty(pe, f"yT{U}", i)
                        transposes(ps[banks.bank[f"yT{U}"]], [yf[u][:, q * P:(q + 1) * P] for q in range(Q)],
                                   L["pe"], f"yT{U}")

            ffn_pe(ffn1)

            G, L = attn["pro"], attn["loop"]

            def bank(X, name, i):
                X["banks"].wait_empty(pe, name, i)
                return ps[X["banks"].bank[name]]

            def three(b, pairs, name, X):
                parts = [p_ for wh_, wl_, mh, ml in pairs for p_ in ((wh_, mh), (wl_, mh), (wh_, ml))]
                for n, (w, m) in enumerate(parts):
                    ins = nc.tensor.matmul(b, w, m, start=(n == 0), stop=(n == len(parts) - 1))
                if name:
                    ins.then_inc(*X["pe"].step(name))

            def norm(X, h, i):
                pe.wait_ge(*X["dve"].done("xn", i))
                transposes(bank(X, f"nT{h}", i), [axn[:, q, :] for q in (2 * h, 2 * h + 1)], X["pe"], f"nT{h}")

            def keys_values(X, c, i):
                own = slice((c % 2) * P, (c % 2 + 1) * P)
                lh, ll = ahh[c // 2][:, own], ahl[c // 2][:, own]
                for w, kind in ((1, "K"), (2, "V")):
                    for h in range(2):
                        cols = slice(w * DA + h * TILE, w * DA + (h + 1) * TILE)
                        three(bank(X, f"{kind}{c}{h}", i)[:, :], [(lh, ll, wah[:, cols], wal[:, cols])], f"{kind}{c}{h}", X)

            def queries(X, name, i):
                h, j = int(name[0]), int(name[1])
                b = bank(X, f"Q{name}", i)
                for n in range(2):
                    cols = slice((2 * j + n) * P, (2 * j + n + 1) * P)
                    three(b[:, n * 2 * P:(n + 1) * 2 * P], [(wah[:, cols], wal[:, cols], ahh[h][:, :], ahl[h][:, :])],
                          f"Q{name}" if n else None, X)

            def transposed_keys(X, c, i):
                for j in range(2):
                    pe.wait_ge(*X["dve"].done(f"phi_K{c}{j}", i))
                    transposes(bank(X, f"KT{c}{j}", i),
                               [kt_[c % 2][:, (4 * j + n) * P:(4 * j + n + 1) * P] for n in range(4)], X["pe"], f"KT{c}{j}")

            def scores(X, c, j, i):
                pe.wait_ge(*X["act"].done(f"kf{c}{j}", i))
                if c % 2 == 0:
                    pe.wait_ge(*X["dve"].done(f"phi_Q{c // 2}{2 * j + 1}", i))
                own = slice((c % 2) * P, (c % 2 + 1) * P)
                ba, bb = bank(X, f"S{c}a{j}", i), bank(X, f"S{c}b{j}", i)
                for n in range(4):
                    p, cols = 4 * j + n, slice(n * P, (n + 1) * P)
                    ia = nc.tensor.matmul(ba[:, cols], kf[0:DH, p, :], qf[c // 2][0:DH, p, own], start=True, stop=True)
                    ib = nc.tensor.matmul(bb[:, cols], kf[DH:P, p, :], qf[c // 2][DH:P, p, own], start=True, stop=True)
                ia.then_inc(*X["pe"].step(f"S{c}a{j}"))
                ib.then_inc(*X["pe"].step(f"S{c}b{j}"))

            all_before(pe, G)
            for h in range(2):
                norm(G, h, 0)
            pe.wait_ge(*G["dve"].done("hl1", 0))
            for j in range(4):
                queries(G, f"0{j}", 0)
            keys_values(G, 0, 0)
            transposed_keys(G, 0, 0)
            scores(G, 0, 0, 0)
            scores(G, 0, 1, 0)
            all_before(pe, L)

            with pe.Fori(0, NT) as i:
                for c in C:
                    k, n = c % 2, (c + 1) % Q
                    if n == 0:
                        pe.wait_ge(*L["dve"].done("hl0", i))
                    keys_values(L, n, i)
                    if c:
                        pe.wait_ge(*L["dve"].done(f"am{c}b1", i))
                    else:
                        pe.wait_ge(*L["dve"].done("am0b1", i, 1))
                        pe.wait_ge(*L["dve"].done("phi_K11", i))
                    own = slice(k * P, (k + 1) * P)
                    for g, (p0, p1) in enumerate(OG):
                        b = bank(L, f"O{c}{g}", i)
                        for p in range(p0, p1):
                            o = (p - p0) * PW
                            nc.tensor.matmul(b[:, o:o + PW], qf[c // 2][:, p, own], state[:, p, :], start=True, stop=False)
                            for m in range(2):
                                ins = nc.tensor.matmul(b[:, o + m * HW:o + (m + 1) * HW], am[:, 2 * (p // 4) + m, p % 4, :],
                                                       vt[k][:, 2 * p + m, :], start=False, stop=(m == 1))
                        ins.then_inc(*L["pe"].step(f"O{c}{g}"))
                        if g < len(QJOBS[c]):
                            queries(L, QJOBS[c][g], i)
                    if c in (1, 3):
                        norm(L, c // 2, i)
                    transposed_keys(L, n, i)
                    for g, (p0, p1) in enumerate(OG):
                        b = bank(L, f"D{c}{g}", i)
                        for p in range(p0, p1):
                            o = (p - p0) * PW
                            ins = nc.tensor.matmul(b[:, o:o + PW], kt_[k][:, p * P:(p + 1) * P],
                                                   vt[k][:, 2 * p:2 * p + 2, :], start=True, stop=True)
                        ins.then_inc(*L["pe"].step(f"D{c}{g}"))
                    pe.wait_ge(*L["dve"].done(f"on{c}2", i))
                    for j in range(2):
                        transposes(bank(L, f"OT{c}{j}", i), [ot[:, 2 * p:2 * p + 2, :] for p in range(4 * j, 4 * j + 4)],
                                   L["pe"], f"OT{c}{j}")
                    scores(L, n, 0, i)
                    if c % 2:
                        pe.wait_ge(*L["dve"].done(f"ol{c}1", i))
                        three(bank(L, f"WO{c // 2}", i)[:, 0:2 * P],
                              [(wah[:, 3 * DA + p * P:3 * DA + (p + 1) * P], wal[:, 3 * DA + p * P:3 * DA + (p + 1) * P],
                                oh[:, p, :], ol[:, p, :]) for p in range(PR)], f"WO{c // 2}", L)
                    scores(L, n, 1, i)
                pe.wait_ge(*L["act"].done("wf1", i))
                transposes(bank(L, "yT", i), [ayf[:, q * P:(q + 1) * P] for q in range(Q)], L["pe"], "yT")

            ffn_pe(ffn2)
            ffn_pe(ffn3)

        @block.scalar
        def _(act):
            def ffn_act(f):
                G, L = f["pro"], f["loop"]
                tern = f["kind"] == "ternary"

                def slot(name):
                    return full[f["splits"].index(name) % NF]

                def slot_free(name, i):
                    k = f["splits"].index(name)
                    if k >= NF:
                        act.wait_ge(*L["pool"].done("lo_" + f["splits"][k - NF], i))
                    else:
                        last = max(j for j in range(len(f["splits"])) if j % NF == k)
                        act.wait_ge(*L["pool"].done("lo_" + f["splits"][last], i, 1))

                def normalised(dst, src):
                    if f["gain"]:
                        return nc.scalar.activation(dst, src, ACT.Identity, scale=f["gain"][0], bias=f["gain"][1])
                    return nc.scalar.copy(dst, src)

                all_before(act, G)
                for u, U in enumerate(PAIR):
                    act.wait_ge(*G["pe"].done(f"nT{U}", 0))
                    normalised(full[u][:, :], ps[u][:, :]).then_inc(*G["act"].step(f"hf{U}"))
                all_before(act, L)

                def norm(u, U, i):
                    act.wait_ge(*L["pe"].done(f"nT{U}", i))
                    slot_free(f"n{U}", i)
                    normalised(slot(f"n{U}")[:, :], ps[f["banks"].bank[f"nT{U}"]][:, :]).then_inc(*L["act"].step(f"hf{U}"))

                def silu(U, i):
                    for m in range(KT):
                        k = f["gates"].index(f"{U}{m}")
                        act.wait_ge(*L["pe"].done(f"g{U}{m}", i))
                        if k >= NS:
                            act.wait_ge(*L["dve"].done("mul" + f["gates"][k - NS], i))
                        else:
                            last = max(j for j in range(len(f["gates"])) if j % NS == k)
                            act.wait_ge(*L["dve"].done("mul" + f["gates"][last], i, 1))
                        nc.scalar.activation(gate[k % NS][:, :], ps[f["banks"].bank[f"g{U}{m}"]][:, :], ACT.Silu,
                                             scale=sc[:, m:m + 1]).then_inc(*L["act"].step(f"silu{U}{m}"))

                def gelu(name, scale, U, i):
                    for m in range(KT):
                        act.wait_ge(*L["pe"].done(f"{name}{U}{m}", i))
                        slot_free(f"{name}{U}{m}", i)
                        s_ = sc[:, scale + m:scale + m + 1] if scale is not None else 1.0
                        nc.scalar.activation(slot(f"{name}{U}{m}")[:, :], ps[f["banks"].bank[f"{name}{U}{m}"]][:, :],
                                             ACT.Gelu, scale=s_).then_inc(*L["act"].step(f"gelu_{name}{U}{m}"))

                def evacuate(u, U, i):
                    act.wait_ge(*L["pe"].done(f"W3{U}", i))
                    act.wait_ge(*L["pe"].done(f"yT{U}", i, 1))
                    nc.scalar.activation(yf[u][:, :], ps[f["banks"].bank[f"W3{U}"]][:, :], ACT.Identity,
                                         scale=s3[:, 0:1] if tern else 1.0).then_inc(*L["act"].step(f"y{U}"))

                with act.Fori(0, NI) as i:
                    if tern:
                        silu("A", i)
                        silu("B", i)
                        norm(0, "A", i)
                        gelu("H1", 2 * KT, "A", i)
                        norm(1, "B", i)
                        gelu("H1", 2 * KT, "B", i)
                        gelu("H2", 3 * KT, "A", i)
                        gelu("H2", 3 * KT, "B", i)
                        evacuate(0, "A", i)
                    else:
                        gelu("L1", None, "A", i)
                        gelu("L1", None, "B", i)
                        norm(0, "A", i)
                        evacuate(0, "A", i)
                        norm(1, "B", i)
                    evacuate(1, "B", i)

            ffn_act(ffn1)

            G, L = attn["pro"], attn["loop"]

            def exp_relu(X, name, i):
                k, src = X["phis"].place[name], ps[X["banks"].bank[name]]
                if X["phis"].prior(name):
                    last, back = X["phis"].prior(name)
                    act.wait_ge(*X["dve"].done(f"phi_{last}", i, back))
                act.wait_ge(*X["pe"].done(name, i))
                nc.scalar.activation(ee[k][:, :], src[:, :], ACT.Exp).then_inc(*X["act"].step(f"e_{name}"))
                nc.scalar.activation(rr[k][:, :], src[:, :], ACT.Relu).then_inc(*X["act"].step(f"r_{name}"))

            def norm(X, h, i):
                act.wait_ge(*X["pe"].done(f"nT{h}", i))
                if X["loop"] or h:
                    act.wait_ge(*X["dve"].done(f"hl{1 - h}", i, 0 if h else 1))
                nc.scalar.activation(ahf[:, :], ps[X["banks"].bank[f"nT{h}"]][:, 0:2 * P], ACT.Identity,
                                     scale=affine[:, 0:1], bias=affine[:, 1:2]).then_inc(*X["act"].step(f"hf{h}"))

            def keys_values(X, c, i):
                for h in range(2):
                    exp_relu(X, f"K{c}{h}", i)
                if X["loop"]:
                    act.wait_ge(*X["pe"].done(f"D{(c - 2) % Q}2", i, 1 if c in (1,) else 0))
                for h in range(2):
                    act.wait_ge(*X["pe"].done(f"V{c}{h}", i))
                    nc.scalar.copy(vt[c % 2][:, h * H // 2:(h + 1) * H // 2, 0:DH],
                                   ps[X["banks"].bank[f"V{c}{h}"]][:, :].rearrange("p (h d) -> p h d", d=DH))\
                        .then_inc(*X["act"].step(f"v{c}{h}"))

            def transposed_keys(X, c, i):
                for j in range(2):
                    act.wait_ge(*X["pe"].done(f"KT{c}{j}", i))
                    nc.scalar.copy(kf[:, 4 * j:4 * j + 4, :],
                                   ps[X["banks"].bank[f"KT{c}{j}"]][:, :].rearrange("p (k n) -> p k n", n=P))\
                        .then_inc(*X["act"].step(f"kf{c}{j}"))

            all_before(act, G)
            for h in range(2):
                norm(G, h, 0)
            for j in range(4):
                exp_relu(G, f"Q0{j}", 0)
            keys_values(G, 0, 0)
            transposed_keys(G, 0, 0)
            all_before(act, L)

            with act.Fori(0, NT) as i:
                for c in C:
                    n = (c + 1) % Q
                    keys_values(L, n, i)
                    if c == 0:
                        act.wait_ge(*L["dve"].done("y", i, 1))
                        nc.scalar.copy(axc[:, :, :], axp[:, :, :]).then_inc(*L["act"].step("cp"))
                    for name in QJOBS[c]:
                        exp_relu(L, f"Q{name}", i)
                    if c in (1, 3):
                        norm(L, c // 2, i)
                    transposed_keys(L, n, i)
                    for j in range(2):
                        act.wait_ge(*L["pe"].done(f"OT{c}{j}", i))
                        if j == 0 and c % 2 == 0:
                            act.wait_ge(*L["pe"].done(f"WO{1 - c // 2}", i, 0 if c else 1))
                        nc.scalar.copy(oh[:, 4 * j:4 * j + 4, (c % 2) * P:(c % 2 + 1) * P],
                                       ps[L["banks"].bank[f"OT{c}{j}"]][:, :].rearrange("p (k n) -> p k n", n=P))\
                            .then_inc(*L["act"].step(f"oh{c}{j}"))
                    if c % 2:
                        h = c // 2
                        act.wait_ge(*L["pe"].done(f"WO{h}", i))
                        if h == 0:
                            act.wait_ge(*L["pe"].done("yT", i, 1))
                        nc.scalar.copy(ayf[:, h * 2 * P:(h + 1) * 2 * P], ps[L["banks"].bank[f"WO{h}"]][:, 0:2 * P])\
                            .then_inc(*L["act"].step(f"wf{h}"))

            ffn_act(ffn2)
            ffn_act(ffn3)

        @block.vector
        def _(dve):
            S = setup["dve"]
            nc.vector.memset(power[:, 0:1], -0.5).then_inc(pe_did, PRIME)
            nc.vector.memset(power[:, 1:2], -0.5).then_inc(act_did, PRIME)
            nc.vector.memset(power[:, 2:3], -0.5).then_inc(pool_did, PRIME)
            nc.vector.memset(power[:, 3:4], -0.5).then_inc(dve_did, PRIME)
            for k, s_ in enumerate((*out_x, out_y, out_xs)):
                nc.vector.memset(spare[:, k + 1:k + 2], 0.0).then_inc(s_, 16)
            nc.vector.memset(s3[:, :], 0.0).then_inc(*S.step("prime"))
            dve.wait_ge(*S.done("prime", 0))
            dve.wait_ge(*setup["pe"].done("vT", 0))
            nc.vector.tensor_copy(sc[:, :], ps[7][:, 0:NV]).then_inc(*S.step("vec"))
            dve.wait_ge(*S.done("vec", 0))
            nc.vector.tensor_scalar(s3[:, :], sc[:, 4 * KT:4 * KT + 1], 0.5, None, ALU.mult).then_inc(*S.step("const"))
            for g, (col, _) in enumerate(groups):
                dve.wait_ge(*setup["pe"].done(f"wT{g}", 0))
                cols = slice(col, col + TILE)
                nc.vector.tensor_copy(wh[:, cols], ps[g % 8][:, :]).then_inc(*S.step(f"hi{g}"))
                dve.wait_ge(*S.done(f"hi{g}", 0))
                nc.vector.tensor_tensor(wl[:, cols], ps[g % 8][:, :], wh[:, cols].bitcast(F32), ALU.subtract)\
                    .then_inc(*S.step(f"lo{g}"))
            dve.wait_ge(in_w, 6 * 16)
            nc.vector.tensor_copy(fh[:, :], sf[:, :]).then_inc(*S.step("fhi"))
            dve.wait_ge(*S.done("fhi", 0))
            nc.vector.tensor_tensor(fl[:, :], sf[:, :], fh[:, :].bitcast(F32), ALU.subtract).then_inc(*S.step("flo"))
            nc.vector.tensor_copy(wah[:, :], sa[:, :]).then_inc(*S.step("ahi"))
            dve.wait_ge(*S.done("ahi", 0))
            nc.vector.tensor_tensor(wal[:, :], sa[:, :], wah[:, :].bitcast(F32), ALU.subtract).then_inc(*S.step("alo"))

            def ffn_dve(f):
                G, L, n = f["pro"], f["loop"], f["n"]
                tern = f["kind"] == "ternary"
                loads = n * (NI + 1)

                def stats(u, U, X, i, arrived):
                    dve.wait_ge(in_ln[u], arrived)
                    for q in range(Q):
                        ins = nc.vector.bn_stats(bst[u][:, q, :], xln[u][:, q, :])
                    ins.then_inc(*X["dve"].step(f"st{U}"))
                    dve.wait_ge(*X["dve"].done(f"st{U}", i))
                    nc.vector.memset(spare[:, 0:1], 0.0)
                    for q in range(Q):
                        ins = nc.vector.bn_aggr(bag[u][:, q, :], bst[u][:, q, :])
                    ins.then_inc(*X["dve"].step(f"ag{U}"))
                    dve.wait_ge(*X["dve"].done(f"ag{U}", i))
                    nc.vector.tensor_scalar(ve[u][:, :], bag[u][:, :, 1], EPS_LN, None, ALU.add)\
                        .then_inc(*X["dve"].step(f"ve{U}"))
                    dve.wait_ge(*X["pool"].done(f"rs{U}", i))
                    if X is L:
                        dve.wait_ge(*X["pe"].done(f"nT{U}", i, 1))
                    for q in range(Q):
                        ins = nc.vector.tensor_scalar(xn[u][:, q, :], xln[u][:, q, :], bag[u][:, q, 0:1],
                                                      rs[u][:, q:q + 1], ALU.subtract, ALU.mult)
                    ins.then_inc(*X["dve"].step(f"xn{U}"))

                def leading(X, name, src, dst, i):
                    nc.vector.tensor_copy(dst, src[:, :]).then_inc(*X["dve"].step(f"hi_{name}"))

                all_before(dve, G)
                for u, U in enumerate(PAIR):
                    stats(u, U, G, 0, 16 * (loads + 1))
                for u, U in enumerate(PAIR):
                    dve.wait_ge(*G["act"].done(f"hf{U}", 0))
                    leading(G, f"n{U}", full[u], nh[u][:, :], 0)
                all_before(dve, L)

                def slot(name):
                    return full[f["splits"].index(name) % NF]

                def slot_free(name, i):
                    k = f["splits"].index(name)
                    if k >= NF:
                        dve.wait_ge(*L["pool"].done("lo_" + f["splits"][k - NF], i))
                    else:
                        last = max(j for j in range(len(f["splits"])) if j % NF == k)
                        dve.wait_ge(*L["pool"].done("lo_" + f["splits"][last], i, 1))

                def norm(u, U, i):
                    dve.wait_ge(*L["act"].done(f"hf{U}", i))
                    dve.wait_ge(*L["pe"].done((f"v{U}{KT - 1}" if tern else f"L1{U}{KT - 1}"), i))
                    leading(L, f"n{U}", slot(f"n{U}"), nh[u][:, :], i)

                def gated(u, U, i):
                    dve.wait_ge(*L["pe"].done(f"W3{U}", i, 1))
                    for m in range(KT):
                        name = f"{U}{m}"
                        k = f["gates"].index(name)
                        dve.wait_ge(*L["pe"].done(f"v{name}", i))
                        dve.wait_ge(*L["act"].done(f"silu{name}", i))
                        slot_free(f"L1{name}", i)
                        nc.vector.scalar_tensor_tensor(slot(f"L1{name}")[:, :], ps[f["banks"].bank[f"v{name}"]][:, :],
                                                       sc[:, KT + m:KT + m + 1], gate[k % NS][:, :], ALU.mult, ALU.mult)\
                            .then_inc(*L["dve"].step(f"mul{name}"))
                        dve.wait_ge(*L["dve"].done(f"mul{name}", i))
                        leading(L, f"L1{name}", slot(f"L1{name}"), ah[u][0][:, m, :], i)

                def activated(name, dst, reader, back, u, U, i):
                    dve.wait_ge(*L["pe"].done(reader, i, back))
                    for m in range(KT):
                        dve.wait_ge(*L["act"].done(f"gelu_{name}{U}{m}", i))
                        leading(L, f"{name}{U}{m}", slot(f"{name}{U}{m}"), ah[u][dst][:, m, :], i)

                with dve.Fori(0, NI) as i:
                    for u, U in enumerate(PAIR):
                        if tern:
                            gated(u, U, i)
                        else:
                            activated("L1", 0, f"W3{U}", 1, u, U, i)
                        stats(u, U, L, i, i * 16 + 16 * (loads + 2))
                    norm(0, "A", i)
                    if tern:
                        activated("H1", 1, f"H2A{KT - 1}", 1, 0, "A", i)
                        norm(1, "B", i)
                        activated("H1", 1, f"H2B{KT - 1}", 1, 1, "B", i)
                        activated("H2", 0, f"H1A{KT - 1}", 0, 0, "A", i)
                        activated("H2", 0, f"H1B{KT - 1}", 0, 1, "B", i)
                    else:
                        norm(1, "B", i)
                    for u, U in enumerate(PAIR):
                        dve.wait_ge(*L["pe"].done(f"yT{U}", i))
                        dve.wait_ge(in_res[u], i * 16 + 16 * (n * NI + 1))
                        dve.wait_ge(out_x[u], i * 16 + 16 * (n * NI + 1))
                        nc.vector.tensor_tensor(xo[u][:, :, :], ps[f["banks"].bank[f"yT{U}"]][:, :].rearrange("p (q d) -> p q d", d=D),
                                                xres[u][:, :, :], ALU.add).then_inc(*L["dve"].step(f"res{U}"))

            ffn_dve(ffn1)

            G, L = attn["pro"], attn["loop"]

            def small(X, name, i, ins):
                ins.then_inc(*X["dve"].step(name))
                dve.wait_ge(*X["dve"].done(name, i))

            def phi(X, name, i):
                if name[0] == "Q":
                    h, j = int(name[1]), int(name[2])
                    dst = qf[h][:, 2 * j:2 * j + 2, :]
                    if X["loop"] and j == 0:
                        dve.wait_ge(*X["pe"].done(f"O{2 * h + 1}2", i, h))
                else:
                    c, h = int(name[1]), int(name[2])
                    dst = kt_[c % 2][:, h * TILE:(h + 1) * TILE]
                    if X["loop"] and h == 0:
                        dve.wait_ge(*X["pe"].done(f"D{(c - 2) % Q}2", i, 1 if c == 1 else 0))
                k = X["phis"].place[name]
                dve.wait_ge(*X["act"].done(f"r_{name}", i))
                nc.vector.scalar_tensor_tensor(dst, ee[k][:, :], 1.0, rr[k][:, :], ALU.min, ALU.add)\
                    .then_inc(*X["dve"].step(f"phi_{name}"))

            def stats(X, i):
                dve.wait_ge(in_ax, i * 16 + (32 if X["loop"] else 16))
                for q in range(Q):
                    ins = nc.vector.bn_stats(abst[:, q, :], ax[:, q, :])
                small(X, "st", i, ins)
                nc.vector.memset(spare[:, 0:1], 0.0)
                for q in range(Q):
                    ins = nc.vector.bn_aggr(abag[:, q, :], abst[:, q, :])
                small(X, "ag", i, ins)
                nc.vector.tensor_scalar(av[:, :], abag[:, :, 1], EPS_LN, None, ALU.add).then_inc(*X["dve"].step("ve"))

            def once(X, i):
                dve.wait_ge(*X["pool"].done("r1", i))
                small(X, "v1", i, nc.vector.tensor_tensor(av1[:, :], abag[:, :, 1], ar1[:, :], ALU.mult))
                small(X, "v2", i, nc.vector.tensor_tensor(av2[:, :], av1[:, :], ar1[:, :], ALU.mult))
                nc.vector.tensor_scalar(av3[:, :], av2[:, :], EPS_LN, None, ALU.add).then_inc(*X["dve"].step("v3"))
                if X["loop"]:
                    dve.wait_ge(*X["act"].done("cp", i))
                for q in range(Q):
                    ins = nc.vector.tensor_scalar(axp[:, q, :], ax[:, q, :], abag[:, q, 0:1], ar1[:, q:q + 1],
                                                  ALU.subtract, ALU.mult)
                ins.then_inc(*X["dve"].step("xp"))

            def twice(X, i):
                dve.wait_ge(*X["pool"].done("r2", i))
                dve.wait_ge(*X["dve"].done("xp", i))
                if X["loop"]:
                    dve.wait_ge(*X["pe"].done("nT1", i, 1))
                for q in range(Q):
                    ins = nc.vector.tensor_scalar(axn[:, q, :], axp[:, q, :], ar2[:, q:q + 1], None, ALU.mult)
                ins.then_inc(*X["dve"].step("xn"))

            def norm(X, h, i):
                dve.wait_ge(*X["act"].done(f"hf{h}", i))
                if X["loop"]:
                    dve.wait_ge(*X["pe"].done(("Q13", "V31")[h] if h else "V11", i, 0))
                nc.vector.tensor_copy(ahh[h][:, :], ahf[:, :]).then_inc(*X["dve"].step(f"hh{h}"))
                dve.wait_ge(*X["dve"].done(f"hh{h}", i))
                nc.vector.tensor_tensor(ahl[h][:, :], ahf[:, :], ahh[h][:, :].bitcast(F32), ALU.subtract)\
                    .then_inc(*X["dve"].step(f"hl{h}"))

            def masked(X, c, j, i):
                for g in ("a", "b"):
                    dve.wait_ge(*X["pe"].done(f"S{c}{g}{j}", i))
                    nc.vector.tensor_tensor(am[:, 2 * j + (g == "b"), :, :],
                                            ps[X["banks"].bank[f"S{c}{g}{j}"]][:, :].rearrange("p (h n) -> p h n", n=P),
                                            mask[:, :, :], ALU.mult).then_inc(*X["dve"].step(f"am{c}{g}{j}"))

            all_before(dve, G)
            for k in range(2):
                nc.vector.memset(vt[k][:, :, DH:DH + 1], 1.0)
                nc.vector.memset(vt[k][:, :, DH + 1:DH + 2], 0.0)
            stats(G, 0)
            once(G, 0)
            twice(G, 0)
            for h in range(2):
                norm(G, h, 0)
            for j in range(4):
                phi(G, f"Q0{j}", 0)
            for h in range(2):
                phi(G, f"K0{h}", 0)
            masked(G, 0, 0, 0)
            masked(G, 0, 1, 0)
            all_before(dve, L)

            with dve.Fori(0, NB) as b_:
                nc.vector.memset(state[:, :, :], 0.0)
                with dve.Fori(0, SUP) as s_:
                    i = b_ * SUP + s_
                    for c in C:
                        n = (c + 1) % Q
                        for h in range(2):
                            phi(L, f"K{n}{h}", i)
                        dve.wait_ge(*L["pe"].done(f"OT{(c - 1) % Q}1", i, 0 if c else 1))
                        for g, (p0, p1) in enumerate(OG):
                            nh_ = 2 * (p1 - p0)
                            src = ps[L["banks"].bank[f"O{c}{g}"]][:, 0:nh_ * HW].rearrange("p (h w) -> p h w", w=HW)
                            dve.wait_ge(*L["pe"].done(f"O{c}{g}", i))
                            small(L, f"dm{c}{g}", i, nc.vector.tensor_scalar(den[:, g, 0:nh_], src[:, :, DH], EPS_DEN, None, ALU.max))
                            small(L, f"rd{c}{g}", i, nc.vector.reciprocal(rden[:, g, 0:nh_], den[:, g, 0:nh_]))
                            nc.vector.tensor_tensor(ot[:, 2 * p0:2 * p1, :], src[:, :, 0:DH],
                                                    rden[:, g, 0:nh_].unsqueeze(2).to_broadcast([P, nh_, DH]), ALU.mult)\
                                .then_inc(*L["dve"].step(f"on{c}{g}"))
                            if g < len(QJOBS[c]):
                                phi(L, f"Q{QJOBS[c][g]}", i)
                        if c == 0:
                            stats(L, i)
                        if c in (1, 3):
                            norm(L, c // 2, i)
                        for g, (p0, p1) in enumerate(OG):
                            src = ps[L["banks"].bank[f"D{c}{g}"]][:, 0:(p1 - p0) * PW].rearrange("p (k w) -> p k w", w=PW)
                            dve.wait_ge(*L["pe"].done(f"D{c}{g}", i))
                            for name, rows, cols in (("sa", slice(0, DH), slice(0, HW)), ("sb", slice(DH, P), slice(HW, PW))):
                                nc.vector.tensor_tensor(state[rows, p0:p1, cols], src[rows, :, cols], state[rows, p0:p1, cols],
                                                        ALU.add).then_inc(*L["dve"].step(f"{name}{c}{g}"))
                        if c == 0:
                            once(L, i)
                        for j in range(2):
                            dve.wait_ge(*L["act"].done(f"oh{c}{j}", i))
                            own = slice((c % 2) * P, (c % 2 + 1) * P)
                            nc.vector.tensor_tensor(ol[:, 4 * j:4 * j + 4, own],
                                                    ps[L["banks"].bank[f"OT{c}{j}"]][:, :].rearrange("p (k n) -> p k n", n=P),
                                                    oh[:, 4 * j:4 * j + 4, own].bitcast(F32), ALU.subtract)\
                                .then_inc(*L["dve"].step(f"ol{c}{j}"))
                        masked(L, n, 0, i)
                        masked(L, n, 1, i)
                        if c == 0:
                            twice(L, i)
                    dve.wait_ge(*L["pe"].done("yT", i))
                    dve.wait_ge(out_y, i * 16 + 16)
                    dve.wait_ge(*L["pool"].done("ys", i, 1))
                    nc.vector.tensor_tensor(ay[:, :, :], ps[L["banks"].bank["yT"]][:, :].rearrange("p (q d) -> p q d", d=D),
                                            axc[:, :, :], ALU.add).then_inc(*L["dve"].step("y"))

            ffn_dve(ffn2)
            ffn_dve(ffn3)

        @block.gpsimd
        def _(pool):
            S = setup["pool"]
            pool.wait_ge(pool_did, PRIME)
            nc.gpsimd.memset(ident[:, :], 0.0).then_inc(*S.step("ones"))
            pool.wait_ge(*S.done("ones", 0))
            nc.gpsimd.affine_select(out=ident[:, :], in_=ident[:, :], compare_op=ALU.not_equal, fill=1.0, base=0,
                                    pattern=[[-1, P]], channel_multiplier=1).then_inc(*S.step("ident"))
            nc.gpsimd.memset(mask[:, :, :], 1.0).then_inc(*S.step("mask1"))
            pool.wait_ge(*S.done("mask1", 0))
            nc.gpsimd.affine_select(out=mask[:, :, :], in_=mask[:, :, :], compare_op=ALU.is_ge, fill=0.0, base=0,
                                    pattern=[[0, 4], [1, P]], channel_multiplier=-1).then_inc(*S.step("mask"))

            def ffn_pool(f):
                G, L = f["pro"], f["loop"]
                tern = f["kind"] == "ternary"

                def rest(X, name, src, hi, dst, i):
                    pool.wait_ge(*X["dve"].done(f"hi_{name}", i))
                    nc.gpsimd.tensor_tensor(dst, src[:, :], hi.bitcast(F32), ALU.subtract)\
                        .then_inc(*X["pool"].step(f"lo_{name}"))

                def rstd(u, U, X, i):
                    pool.wait_ge(*X["dve"].done(f"ve{U}", i))
                    nc.gpsimd.tensor_tensor(rs[u][:, :], ve[u][:, :], power[:, :], ALU.pow).then_inc(*X["pool"].step(f"rs{U}"))

                all_before(pool, G)
                for u, U in enumerate(PAIR):
                    rstd(u, U, G, 0)
                for u, U in enumerate(PAIR):
                    rest(G, f"n{U}", full[u], nh[u][:, :], nl[u][:, :], 0)
                all_before(pool, L)

                def slot(name):
                    return full[f["splits"].index(name) % NF]

                def layer(name, dst, u, U, i):
                    for m in range(KT):
                        rest(L, f"{name}{U}{m}", slot(f"{name}{U}{m}"), ah[u][dst][:, m, :], al[u][dst][:, m, :], i)

                def norm(u, U, i):
                    rest(L, f"n{U}", slot(f"n{U}"), nh[u][:, :], nl[u][:, :], i)

                with pool.Fori(0, NI) as i:
                    for u, U in enumerate(PAIR):
                        layer("L1", 0, u, U, i)
                        rstd(u, U, L, i)
                    norm(0, "A", i)
                    if tern:
                        layer("H1", 1, 0, "A", i)
                        norm(1, "B", i)
                        layer("H1", 1, 1, "B", i)
                        layer("H2", 0, 0, "A", i)
                        layer("H2", 0, 1, "B", i)
                    else:
                        norm(1, "B", i)

            ffn_pool(ffn1)

            G, L = attn["pro"], attn["loop"]

            def root(X, name, after, dst, src, i):
                pool.wait_ge(*X["dve"].done(after, i))
                nc.gpsimd.tensor_tensor(dst[:, :], src[:, :], power[:, :], ALU.pow).then_inc(*X["pool"].step(name))

            all_before(pool, G)
            root(G, "r1", "ve", ar1, av, 0)
            root(G, "r2", "v3", ar2, av3, 0)
            all_before(pool, L)
            with pool.Fori(0, NT) as i:
                root(L, "r1", "ve", ar1, av, i)
                root(L, "r2", "v3", ar2, av3, i)
                pool.wait_ge(*L["dve"].done("y", i))
                pool.wait_ge(in_ar, i * 16 + 16)
                pool.wait_ge(out_xs, i * 16 + 16)
                nc.gpsimd.tensor_tensor(axs[:, :, :], ay[:, :, :], axr[:, :, :], ALU.add).then_inc(*L["pool"].step("ys"))

            ffn_pool(ffn2)
            ffn_pool(ffn3)


_INS = ["L0_attn_x", "L0_attn_ln1_g", "L0_attn_ln1_b", "L0_attn_Wq", "L0_attn_Wk", "L0_attn_Wv", "L0_attn_Wo",
        "L0_attn_ln2_g", "L0_attn_ln2_b", "L0_attn_Wf1", "L0_attn_Wf2", "L0_ffn_w1_w", "L0_ffn_w1_s", "L0_ffn_w2_w",
        "L0_ffn_w2_s", "L0_ffn_h1_w", "L0_ffn_h1_s", "L0_ffn_h2_w", "L0_ffn_h2_s", "L0_ffn_w3_w", "L0_ffn_w3_s"]


def kernel(**inputs):
    import numpy as np
    import concourse.bacc as bacc
    from concourse.bass_utils import run_bass_kernel_spmd

    nc = bacc.Bacc("TRN2", target_bir_lowering=False, num_devices=1)
    arrays, args = {}, {}
    for name in _INS:
        a = np.ascontiguousarray(inputs[name])
        arrays[f"in_{name}"] = a
        args[name] = nc.dram_tensor(f"in_{name}", a.shape, mybir.dt.from_np(a.dtype), kind="ExternalInput").ap()
    x = arrays["in_L0_attn_x"]
    out = nc.dram_tensor("out_0", x.shape, mybir.dt.from_np(x.dtype), kind="ExternalOutput").ap()
    build_kernel(nc, args, out.rearrange("b t d -> (b t) d"))
    got = run_bass_kernel_spmd(nc, [arrays], core_ids=[0])
    return got.results[0]["out_0"]
```

```python
from contextlib import ExitStack

import concourse.bass as bass
from concourse import mybir

P = 128
ALU = mybir.AluOpType
ACT = mybir.ActivationFunctionType
F32 = mybir.dt.float32
F32R = mybir.dt.float32r
EPS_LN = 1e-5
EPS_DEN = 1e-6

TILE = 512
Q = TILE // P
PAIR = ("A", "B")


class Steps:

    def __init__(self, sem, base, names):
        assert len(set(names)) == len(names)
        self.sem, self.base, self.names = sem, base, names
        self.at = {name: n + 1 for n, name in enumerate(names)}
        self.next = 0

    def step(self, name):
        assert self.names[self.next % len(self.names)] == name, (name, self.names[self.next % len(self.names)])
        self.next += 1
        return self.sem, 1

    def done(self, name, i, back=0):
        return self.sem, i * len(self.names) + (self.base + self.at[name] - back * len(self.names))

    def end(self, iterations):
        return self.base + iterations * len(self.names)


class Ring:

    def __init__(self, jobs, size, loop=True):
        self.place, self.before = {}, {}
        for n, job in enumerate(jobs):
            self.place[job] = n % size
            if n >= size:
                self.before[job] = (jobs[n - size], 0)
            elif loop:
                self.before[job] = (jobs[max(j for j in range(len(jobs)) if j % size == n)], 1)
            else:
                self.before[job] = None

    def prior(self, job):
        return self.before[job]


class Banks:

    def __init__(self, jobs, loop=True):
        self.bank = {job: bank for job, bank, _, _ in jobs}
        self.prior = {}
        for n, (job, bank, _, _) in enumerate(jobs):
            same = [k for k, j in enumerate(jobs) if j[1] == bank]
            before = [k for k in same if k < n]
            if before or loop:
                k = before[-1] if before else same[-1]
                self.prior[job] = (jobs[k][2], jobs[k][3], 0 if before else 1)

    def wait_empty(self, eng, job, i):
        if job in self.prior:
            steps, name, back = self.prior[job]
            eng.wait_ge(*steps.done(name, i, back))


def build_kernel(nc, t, out):
    x_in = t["L0_attn_x"].rearrange("b t d -> (b t) d")
    NTOK, D = x_in.shape
    DH_ = t["plain"].shape[1] // 2
    KT = DH_ // P
    DA = t["attn"].shape[2]
    DH = 64
    H = DA // DH
    PR = H // 2
    NB = t["L0_attn_x"].shape[0]
    NT = NTOK // TILE
    NI = NT // 2
    SUP = NT // NB
    HW = DH + 2
    PW = 2 * HW
    OG = [(0, 3), (3, 6), (6, 8)]
    assert D == P and NTOK % (2 * TILE) == 0 and H == 16 and KT == 4

    W1, W2, H1, H2, W3 = 0, DH_, 2 * DH_, 2 * DH_ + KT * DH_, 2 * DH_ + 2 * KT * DH_
    WCOLS = W3 + DH_
    assert t["ternary"].shape == (P, WCOLS)
    PIECES = [(W1, H1), (H1, H1 + 2 * DH_), (H1 + 2 * DH_, H2), (H2, H2 + 2 * DH_), (H2 + 2 * DH_, W3), (W3, WCOLS)]
    NPC = len(PIECES)

    ctx = ExitStack()

    def sem(name):
        return ctx.enter_context(nc.semaphore(name))

    def sb(stack, name, shape, dt=F32):
        return stack.enter_context(nc.sbuf_tensor(name, shape, dt))

    def view(dram):
        return dram.rearrange("(n q p) d -> n p q d", q=Q, p=P)

    with ctx:
        ident = sb(ctx, "ident", [P, P])
        mask = sb(ctx, "mask", [P, 4, P])
        wh = sb(ctx, "wh", [P, WCOLS], F32R)
        wl = sb(ctx, "wl", [P, WCOLS], F32R)
        fh = sb(ctx, "fh", [P, 2 * DH_], F32R)
        fl = sb(ctx, "fl", [P, 2 * DH_], F32R)
        wah = sb(ctx, "wah", [P, 4 * DA], F32R)
        wal = sb(ctx, "wal", [P, 4 * DA], F32R)
        NV = 4 * KT + 5
        sc = sb(ctx, "sc", [P, NV])
        s3 = sb(ctx, "s3", [P, 1])
        affine = sc[:, NV - 4:NV]
        spare = sb(ctx, "spare", [P, 5])
        warm = sb(ctx, "warm", [P, 2])
        power = sb(ctx, "power", [P, Q])
        x1_d = nc.dram_tensor("x1_scratch", (NTOK, D), F32).ap()
        yx2_d = nc.dram_tensor("yx2_scratch", (2 * NTOK, D), F32).ap()
        y_d, x2_d = yx2_d[0:NTOK, :], yx2_d[NTOK:2 * NTOK, :]
        xs_d = nc.dram_tensor("xs_scratch", (NTOK, D), F32).ap()
        ps = [ctx.enter_context(nc.psum_tensor(f"ps{b}", [P, TILE], F32)) for b in range(8)]

        stage = sb(ctx, "stage", [P, DA])
        rest_sum = sb(ctx, "rest_sum", [P, NPC])
        ones = sb(ctx, "ones", [P, 1])
        flag = sb(ctx, "flag", [1, 1])

        xln = [sb(ctx, f"xln{u}", [P, Q, D]) for u in PAIR]
        xn = [sb(ctx, f"xn{u}", [P, Q, D]) for u in PAIR]
        xo = [sb(ctx, f"xo{u}", [P, Q, D]) for u in PAIR]
        bst = [sb(ctx, f"bst{u}", [P, Q, 6]) for u in PAIR]
        bag = [sb(ctx, f"bag{u}", [P, Q, 2]) for u in PAIR]
        ve = [sb(ctx, f"ve{u}", [P, Q]) for u in PAIR]
        rs = [sb(ctx, f"rs{u}", [P, Q]) for u in PAIR]
        abst = sb(ctx, "abst", [P, Q, 6])
        abag = sb(ctx, "abag", [P, Q, 2])
        av, ar1 = sb(ctx, "av", [P, Q]), sb(ctx, "ar1", [P, Q])
        ax = xln[0]

        with ExitStack() as s:
            xres = [sb(s, f"xres{u}", [P, Q, D]) for u in PAIR]
            nh = [sb(s, f"nh{u}", [P, TILE], F32R) for u in PAIR]
            nl = [sb(s, f"nl{u}", [P, TILE], F32R) for u in PAIR]
            NF = 6
            full = [sb(s, f"full{k}", [P, TILE]) for k in range(NF)]
            NS = 3
            gate = [sb(s, f"gate{k}", [P, TILE]) for k in range(NS)]
            yf = [sb(s, f"yf{u}", [P, TILE]) for u in PAIR]
            with ExitStack() as s2:
                wst = sb(s2, "wst", [P, WCOLS])
                sf = sb(s2, "sf", [P, 2 * DH_])
                junk = sb(s2, "junk", [P, 2 * DH_])
            ah = [[sb(s, f"ah{u}{k}", [P, KT, TILE], F32R) for k in range(2)] for u in PAIR]
            al = [[sb(s, f"al{u}{k}", [P, KT, TILE], F32R) for k in range(2)] for u in PAIR]

        with ExitStack() as s:
            axr = sb(s, "axr", [P, Q, D])
            axp = sb(s, "axp", [P, Q, D])
            axc = sb(s, "axc", [P, Q, D])
            axn = sb(s, "axn", [P, Q, D])
            ahh = [sb(s, f"ahh{h}", [P, TILE // 2], F32R) for h in range(2)]
            ahl = [sb(s, f"ahl{h}", [P, TILE // 2], F32R) for h in range(2)]
            ahf = sb(s, "ahf", [P, TILE // 2])
            qf = [sb(s, f"qf{h}", [P, PR, TILE // 2]) for h in range(2)]
            kt_ = [sb(s, f"kt{k}", [P, DA]) for k in range(2)]
            vt = [sb(s, f"vt{k}", [P, H, HW]) for k in range(2)]
            kf = sb(s, "kf", [P, PR, P])
            am = sb(s, "am", [P, 4, 4, P])
            state = sb(s, "state", [P, PR, PW])
            ot = sb(s, "ot", [P, H, DH])
            oh = sb(s, "oh", [P, PR, TILE // 2], F32R)
            ol = sb(s, "ol", [P, PR, TILE // 2], F32R)
            NE = 2
            ee = [sb(s, f"ee{k}", [P, TILE]) for k in range(NE)]
            rr = [sb(s, f"rr{k}", [P, TILE]) for k in range(NE)]
            den = sb(s, "den", [P, 3, 6])
            rden = sb(s, "rden", [P, 3, 6])
            ayf = sb(s, "ayf", [P, TILE])
            ay = sb(s, "ay", [P, Q, D])
            axs = sb(s, "axs", [P, Q, D])
            av1, av2, av3, ar2 = (sb(s, f"as{k}", [P, Q]) for k in range(4))

        pe_did, act_did, dve_did, pool_did = sem("pe_did"), sem("act_did"), sem("dve_did"), sem("pool_did")
        in_w = [sem(f"in_w{k}") for k in range(NPC)]
        in_f, in_v = sem("in_f"), sem("in_v")
        in_a = sem("in_a")
        in_ln = [sem(f"in_ln{u}") for u in PAIR]
        in_res = [sem(f"in_res{u}") for u in PAIR]
        out_x = [sem(f"out_x{u}") for u in PAIR]
        in_ar = sem("in_ar")
        in_ax, out_y, out_xs = sem("in_ax"), sem("out_y"), sem("out_xs")

        PRIME = 1024
        ENG = ("pe", "act", "dve", "pool")
        sems = dict(pe=pe_did, act=act_did, dve=dve_did, pool=pool_did)
        base = dict.fromkeys(ENG, PRIME)
        plan = []

        def phase(iterations, **names):
            steps = {e: Steps(sems[e], base[e], names.get(e, [])) for e in ENG}
            for e in ENG:
                base[e] = steps[e].end(iterations)
            plan.append(steps)
            return steps

        def all_before(eng, steps):
            for e in ENG:
                eng.wait_ge(steps[e].sem, steps[e].base)

        setup = phase(1, dve=["prime", "s3"], pool=["id0", "ident", "ones", "mask1", "mask"])

        LAYERS = {"ternary": ["L1", "H1", "H2", "W3"], "plain": ["L1", "W3"]}
        STATS = ("st", "ag", "ve")

        def hi_by(kind, name):
            return "act" if name[0] == "n" or (kind == "plain" and int(name[-1]) % 2) else "dve"

        def lo_by(kind, name):
            if name[0] == "n" or (kind == "ternary" and name[:2] == "L1"):
                return "pool"
            return "dve" if int(name[-1]) == KT - 1 or (kind == "plain" and int(name[-1]) % 2) else "pool"

        def prologue(normalised=False):
            made = [] if normalised else ["rsA", "rsB"]
            return phase(1, pe=["nTA", "nTB"], act=["hfA", "hi_nA", "hfB", "hi_nB"],
                         dve=[] if normalised else [f"{n}{u}" for u in PAIR for n in STATS] + ["xnA", "xnB"],
                         pool=made + ["lo_nA", "lo_nB"])

        def ffn_plan(kind, pro, splits_attention=False):
            tern = kind == "ternary"
            pe, act, dve, pool, splits, gates = [], [], [], [], [], []
            by_engine = dict(act=act, dve=dve, pool=pool)

            def split(name):
                splits.append(name)
                by_engine[hi_by(kind, name)].append(f"hi_{name}")
                by_engine[lo_by(kind, name)].append(f"lo_{name}")

            def job(name, u, m):
                if name == "L1" and tern:
                    pe.extend([f"g{u}{m}", f"v{u}{m}"])
                    act.append(f"silu{u}{m}")
                    gates.append(f"{u}{m}")
                    dve.append(f"mul{u}{m}")
                else:
                    pe.append(f"{name}{u}{m}")
                    act.append(f"gelu_{name}{u}{m}")
                split(f"{name}{u}{m}")

            def layer(name, u):
                for m in range(KT):
                    job(name, u, m)

            def stats(u):
                dve.extend(f"{n}{u}" for n in STATS)

            def norm(u):
                pe.append(f"nT{u}")
                act.append(f"hf{u}")
                split(f"n{u}")

            if tern:
                layer("L1", "A")
                layer("L1", "B")
                for u in PAIR:
                    for m in range(KT):
                        job("H1", u, m)
                        if m == 1:
                            stats(u)
                        if m == 2:
                            pool.append(f"rs{u}")
                    dve.append(f"xn{u}")
                norm("A")
                for m in range(KT):
                    job("H2", "A", m)
                    if splits_attention and m in (1, 2):
                        dve.append(("ahi", "alo")[m - 1])
                layer("H2", "B")
                pe.append("W3A")
                act.append("yA")
                norm("B")
                pe.extend(["W3B", "yTA", "yTB"])
                act.append("yB")
                dve.extend(["resA", "resB"])
            else:
                for u in PAIR:
                    if u == "A":
                        stats(u)
                    for m in range(KT):
                        job("L1", u, m)
                        if u == "A" and m == 0:
                            pool.append("rsA")
                    if u == "B":
                        stats(u)
                        pool.append("rsB")
                    dve.append(f"xn{u}")
                pe.append("W3A")
                act.append("yA")
                norm("A")
                pe.extend(["W3B", "yTA", "yTB"])
                act.append("yB")
                norm("B")
                dve.extend(["resA", "resB"])
            loop = phase(NI, pe=pe, act=act, dve=dve, pool=pool)
            A, V = loop["act"], loop["dve"]
            jobs, n = [], 0
            for name in pe:
                if name[:2] == "nT":
                    jobs.append((name, 6, A, "hi_n" + name[2]))
                elif name[:2] == "yT":
                    jobs.append((name, 7 if tern or name[2] == "B" else 5, V, "res" + name[2]))
                else:
                    if name[:2] == "W3":
                        by = (A, "y" + name[2])
                    elif name[0] == "g":
                        by = (A, "silu" + name[1:])
                    elif name[0] == "v":
                        by = (V, "mul" + name[1:])
                    elif hi_by(kind, name) == "act":
                        by = (A, "hi_" + name)
                    else:
                        by = (A, "gelu_" + name)
                    jobs.append((name, n % (6 if tern else 5), *by))
                    n += 1
            return dict(kind=kind, pro=pro, loop=loop, banks=Banks(jobs), splits=splits, gates=gates)

        def split_done(f, X, name, i, back=0):
            return X[lo_by(f["kind"], name)].done("lo_" + name, i, back)

        def slot(f, name):
            return full[f["splits"].index(name) % NF]

        def slot_free(eng, f, name, i):
            k = f["splits"].index(name)
            last = k - NF if k >= NF else max(j for j in range(len(f["splits"])) if j % NF == k)
            eng.wait_ge(*split_done(f, f["loop"], f["splits"][last], i, 0 if k >= NF else 1))

        pro1 = prologue()
        LO_BY_POOL = (1,)
        weights = phase(1, pe=["flag"], act=[f"sum{k}" for k in range(NPC)],
                        dve=[f"{w}{k}" for k in range(NPC) for w in ("hi", "lo") if w == "hi" or k not in LO_BY_POOL]
                        + ["fhi", "flo", "flag"], pool=[f"lo{k}" for k in LO_BY_POOL])
        ffn1 = ffn_plan("ternary", pro1, True)

        C = range(Q)
        SG = ("a0", "b0", "a1", "b1")

        def attention_plan():
            lists = {}
            for part in ("pro", "loop"):
                pe, act, dve, pool, phis, jobs, count = [], [], [], [], [], [], {"P": 0, "O": 0}

                def job(ring, name, eng, by):
                    pe.append(name)
                    jobs.append((name, count[ring] % 2 + (0 if ring == "P" else 6), eng, by))
                    count[ring] += 1

                def phi(name):
                    phis.append(name)
                    job("P", name, "act", f"r_{name}")
                    act.extend([f"e_{name}", f"r_{name}"])
                    dve.append(f"phi_{name}")

                def values(c, h):
                    job("P", f"V{c}{h}", "act", f"v{c}{h}")
                    act.append(f"v{c}{h}")

                def norm(h):
                    job("P", f"nT{h}", "act", f"hf{h}")
                    act.append(f"hf{h}")
                    dve.extend([f"hh{h}", f"hl{h}"])

                def kt(c):
                    for j in range(2):
                        job("P", f"KT{c}{j}", "act", f"kf{c}{j}")
                        act.append(f"kf{c}{j}")

                def scores(c, j):
                    for g in ("a", "b"):
                        pe.append(f"S{c}{g}{j}")
                        jobs.append((f"S{c}{g}{j}", 2 + 2 * j + (g == "b"), "dve", f"am{c}{g}{j}"))
                        dve.append(f"am{c}{g}{j}")

                if part == "pro":
                    dve.extend(["st", "ag", "ve", "v1", "v2", "v3", "xp", "xn"])
                    pool.extend(["r1", "r2"])
                    norm(0)
                    norm(1)
                    for j in range(4):
                        phi(f"Q0{j}")
                    phi("K00")
                    phi("K01")
                    values(0, 0)
                    values(0, 1)
                    kt(0)
                    scores(0, 0)
                    scores(0, 1)
                else:
                    for c in C:
                        n = (c + 1) % Q
                        qs = QJOBS[c]
                        for h in range(2):
                            phi(f"K{n}{h}")
                            if c == 0:
                                values(n, h)
                        if c == 0:
                            act.append("cp")
                        for g in range(3):
                            job("O", f"O{c}{g}", "dve", f"on{c}{g}")
                            dve.extend([f"dm{c}{g}", f"rd{c}{g}", f"on{c}{g}"])
                            if g < len(qs):
                                phi(f"Q{qs[g]}")
                                if c:
                                    values(n, g)
                            if c == 1 and g == 0:
                                dve.extend(["v1", "v2", "v3", "xp"])
                                pool.append("r2")
                        kt(n)
                        if c == 1:
                            dve.append("xn")
                        for g in range(3):
                            job("O", f"D{c}{g}", "dve", f"sb{c}{g}")
                            dve.extend([f"sa{c}{g}", f"sb{c}{g}"])
                            if c % 2 and g == 1:
                                job("P", f"nT{c // 2}", "act", f"hf{c // 2}")
                                act.append(f"hf{c // 2}")
                        if c == 0:
                            dve.extend(["st", "ag", "ve"])
                            pool.append("r1")
                        for j in range(2):
                            job("P", f"OT{c}{j}", "dve", f"ol{c}{j}")
                            act.append(f"oh{c}{j}")
                            dve.append(f"ol{c}{j}")
                        if c % 2:
                            scores(n, 0)
                            job("P", f"WO{c // 2}", "act", f"wf{c // 2}")
                            act.append(f"wf{c // 2}")
                            scores(n, 1)
                        else:
                            scores(n, 0)
                            scores(n, 1)
                        if c % 2:
                            dve.extend([f"hh{c // 2}", f"hl{c // 2}"])
                    pe.append("yT")
                    jobs.append(("yT", 6, "dve", "y"))
                    dve.append("y")
                    pool.append("ys")
                lists[part] = (pe, act, dve, pool, phis, jobs)
            made = {}
            for part, its in (("pro", 1), ("loop", NT)):
                pe, act, dve, pool, phis, jobs = lists[part]
                X = phase(its, pe=pe, act=act, dve=dve, pool=pool)
                X["loop"] = part == "loop"
                X["phis"] = Ring(phis, NE, part == "loop")
                X["banks"] = Banks([(j, b, X[e], by) for j, b, e, by in jobs], part == "loop")
                made[part] = X
            return made

        QJOBS = (("10", "11"), ("12", "13"), ("00", "01"), ("02", "03"))
        attn = attention_plan()
        ffn2 = ffn_plan("plain", prologue())
        ffn3 = ffn_plan("ternary", prologue(normalised=True))
        ffn1.update(loads=0)
        ffn2.update(loads=NI + 1)
        ffn3.update(loads=2 * NI + 3)
        ffn1.update(n=0, ln=x_in, res=x_in, dst=x1_d, hi=wh, lo=wl, gain=None)
        ffn2.update(n=1, ln=yx2_d, res=xs_d, dst=x2_d, hi=fh, lo=fl, gain=(affine[:, 2:3], affine[:, 3:4]))
        ffn3.update(n=2, ln=x2_d, res=x2_d, dst=out, hi=wh, lo=wl, gain=None)

        block = ctx.enter_context(nc.Block())

        @block.sync
        def _(sp):
            sp.dma_start(sc[:, :], t["vectors"]).then_inc(in_v, 16)
            for u in range(2):
                sp.dma_start(xln[u][:, :, :], view(x_in)[u]).then_inc(in_ln[u], 16)
            for k, (a, b) in enumerate(PIECES):
                sp.dma_start(wst[:, a:b], t["ternary"][:, a:b]).then_inc(in_w[k], 16)
            sp.dma_start(sf[:, :], t["plain"]).then_inc(in_f, 16)

            def ffn_dma(f):
                n, V, PV = f["n"], f["loop"]["dve"], f["pro"]["dve"]
                src, res = view(f["ln"]), view(f["res"])
                dst = f["dst"].rearrange("(i u q p) d -> i u p q d", u=2, q=Q, p=P)
                if n < 2:
                    for u, U in enumerate(PAIR):
                        sp.wait_ge(*PV.done(f"xn{U}", 0))
                        sp.dma_start(xln[u][:, :, :], src[2 + u]).then_inc(in_ln[u], 16)
                if n:
                    all_before(sp, f["loop"])

                def transfers(i, ahead):
                    if n == 0:
                        sp.wait_ge(*V.done("alo", i, 1))
                        sp.dma_start(stage[:, :], t["attn"][i]).then_inc(in_a, 16)
                    for u, U in enumerate(PAIR):
                        sp.wait_ge(*V.done(f"res{U}", i, 1))
                        sp.dma_start(xres[u][:, :, :], res[i * 2 + u]).then_inc(in_res[u], 16)
                    if ahead is not None:
                        tiles = [src[ahead * 2 + u] for u in range(2)]
                        for u, U in enumerate(PAIR):
                            sp.wait_ge(*V.done(f"xn{U}", i))
                            sp.dma_start(xln[u][:, :, :], tiles[u]).then_inc(in_ln[u], 16)
                    elif n == 0:
                        sp.wait_ge(*V.done("xnA", i))
                        sp.dma_start(ax[:, :, :], view(x1_d)[0]).then_inc(in_ax, 16)
                    for u, U in enumerate(PAIR):
                        sp.wait_ge(*V.done(f"res{U}", i))
                        sp.dma_start(dst[i, u], xo[u][:, :, :]).then_inc(out_x[u], 16)

                if n == 1:
                    with sp.Fori(0, NI) as i:
                        transfers(i, i + 2)
                else:
                    with sp.Fori(0, NI - 1) as i:
                        transfers(i, (i + 2) % NI)
                    transfers(NI - 1, None)
                for u in range(2):
                    sp.wait_ge(out_x[u], 16 * NI * (n + 1) + 16)

            ffn_dma(ffn1)

            L = attn["loop"]
            all_before(sp, L)

            def attention_transfers(i, ahead, final=False):
                sp.wait_ge(*L["dve"].done("xp", i, 1))
                sp.dma_start(ax[:, :, :], view(x1_d)[ahead]).then_inc(in_ax, 16)
                sp.wait_ge(*L["pool"].done("ys", i, 1))
                sp.dma_start(axr[:, :, :], view(x1_d)[i]).then_inc(in_ar, 16)
                if final:
                    sp.wait_ge(*L["dve"].done("xp", i))
                    for u in range(2):
                        sp.dma_start(xln[u][:, :, :], view(yx2_d)[u]).then_inc(in_ln[u], 16)
                sp.wait_ge(*L["dve"].done("y", i))
                sp.dma_start(view(y_d)[i], ay[:, :, :]).then_inc(out_y, 16)
                sp.wait_ge(*L["pool"].done("ys", i))
                sp.dma_start(view(xs_d)[i], axs[:, :, :]).then_inc(out_xs, 16)

            with sp.Fori(0, NT - 1) as i:
                attention_transfers(i, i + 1)
            attention_transfers(NT - 1, 0, final=True)
            sp.wait_ge(out_y, 16 * NT + 16)
            sp.wait_ge(out_xs, 16 * NT + 16)

            ffn_dma(ffn2)
            ffn_dma(ffn3)

        @block.tensor
        def _(pe):
            def transposes(dst, sources, steps, name):
                for k, src in enumerate(sources):
                    ins = nc.tensor.transpose(dst[:, k * P:(k + 1) * P], src, ident[:, :])
                ins.then_inc(*steps.step(name))

            more_bits = []

            def ffn_pe(f):
                kind, banks, L = f["kind"], f["banks"], f["loop"]
                G = f["pro"]
                all_before(pe, G)
                for u, U in enumerate(PAIR):
                    if f["n"] < 2:
                        pe.wait_ge(*G["dve"].done(f"xn{U}", 0))
                    transposes(ps[u], [xn[u][:, q, :] for q in range(Q)], G["pe"], f"nT{U}")
                if f["n"] == 0:
                    W = weights
                    pe.wait_ge(*W["act"].done(f"sum{NPC - 1}", 0))
                    nc.tensor.matmul(ps[7][0:1, 0:NPC], ones[:, 0:1], rest_sum[:, :], start=True, stop=True)\
                        .then_inc(*W["pe"].step("flag"))
                    pe.wait_ge(*W["dve"].done("flag", 0))
                    more_bits.append(pe.value_load(flag[0:1, 0:1].bitcast(mybir.dt.int32)))
                all_before(pe, L)

                def product(name, i, col, hi_in, lo_in, ks):
                    banks.wait_empty(pe, name, i)
                    b = ps[banks.bank[name]]
                    parts = [(k, xp_, w) for k in ks for xp_, w in ((hi_in, f["hi"]), (lo_in, f["hi"]), (hi_in, f["lo"]))[:terms[0]]]
                    for n, (k, x_, w) in enumerate(parts):
                        ins = nc.tensor.matmul(b[:, :], w[:, col(k):col(k) + P], x_[:, k, :],
                                               start=(n == 0), stop=(n == len(parts) - 1))
                    ins.then_inc(*L["pe"].step(name))

                def norm(u, U, i):
                    pe.wait_ge(*L["dve"].done(f"xn{U}", i))
                    banks.wait_empty(pe, f"nT{U}", i)
                    transposes(ps[banks.bank[f"nT{U}"]], [xn[u][:, q, :] for q in range(Q)], L["pe"], f"nT{U}")

                def first(u, U, i):
                    hi_in, lo_in = (a[u][:, :].rearrange("p (k n) -> p k n", k=1) for a in (nh, nl))
                    pe.wait_ge(*split_done(f, L, f"n{U}", i, 1))
                    for m in range(KT):
                        if kind == "ternary":
                            product(f"g{U}{m}", i, lambda k: W1 + m * P, hi_in, lo_in, [0])
                            product(f"v{U}{m}", i, lambda k: W2 + m * P, hi_in, lo_in, [0])
                        else:
                            product(f"L1{U}{m}", i, lambda k: m * P, hi_in, lo_in, [0])

                def inputs(before, U, i):
                    for m in (KT - 2, KT - 1):
                        pe.wait_ge(*split_done(f, L, f"{before}{U}{m}", i))

                def hidden(name, before, off, src, u, U, i):
                    inputs(before, U, i)
                    for m in range(KT):
                        product(f"{name}{U}{m}", i, lambda k: off + k * DH_ + m * P, ah[u][src], al[u][src], range(KT))

                def last(before, off, src, u, U, i):
                    inputs(before, U, i)
                    product(f"W3{U}", i, lambda k: off + k * P, ah[u][src], al[u][src], range(KT))

                def iteration(i):
                    first(0, "A", i)
                    first(1, "B", i)
                    if kind == "ternary":
                        hidden("H1", "L1", H1, 0, 0, "A", i)
                        hidden("H1", "L1", H1, 0, 1, "B", i)
                        norm(0, "A", i)
                        hidden("H2", "H1", H2, 1, 0, "A", i)
                        hidden("H2", "H1", H2, 1, 1, "B", i)
                        last("H2", W3, 0, 0, "A", i)
                        norm(1, "B", i)
                        last("H2", W3, 0, 1, "B", i)
                    else:
                        last("L1", DH_, 0, 0, "A", i)
                        norm(0, "A", i)
                        last("L1", DH_, 0, 1, "B", i)
                    for u, U in enumerate(PAIR):
                        pe.wait_ge(*L["act"].done(f"y{U}", i))
                        banks.wait_empty(pe, f"yT{U}", i)
                        transposes(ps[banks.bank[f"yT{U}"]], [yf[u][:, q * P:(q + 1) * P] for q in range(Q)],
                                   L["pe"], f"yT{U}")
                    if kind == "plain":
                        norm(1, "B", i)

                terms = [3]
                if kind == "ternary":
                    with pe.If(more_bits[0] != 0):
                        with pe.Fori(0, NI) as i:
                            iteration(i)
                    with pe.Else():
                        terms[0] = 2
                        with pe.Fori(0, NI) as i:
                            iteration(i)
                else:
                    with pe.Fori(0, NI) as i:
                        iteration(i)

            ffn_pe(ffn1)

            G, L = attn["pro"], attn["loop"]

            def bank(X, name, i):
                X["banks"].wait_empty(pe, name, i)
                return ps[X["banks"].bank[name]]

            def three(b, pairs, name, X):
                parts = [p_ for wh_, wl_, mh, ml in pairs for p_ in ((wh_, mh), (wl_, mh), (wh_, ml))]
                for n, (w, m) in enumerate(parts):
                    ins = nc.tensor.matmul(b, w, m, start=(n == 0), stop=(n == len(parts) - 1))
                if name:
                    ins.then_inc(*X["pe"].step(name))

            def norm(X, h, i):
                pe.wait_ge(*X["dve"].done("xn", i))
                transposes(bank(X, f"nT{h}", i), [axn[:, q, :] for q in (2 * h, 2 * h + 1)], X["pe"], f"nT{h}")

            def token_major(X, kind, c, h, i):
                own = slice((c % 2) * P, (c % 2 + 1) * P)
                lh, ll = ahh[c // 2][:, own], ahl[c // 2][:, own]
                first = {"K": 1, "V": 2}[kind] * DA + h * TILE
                cols = slice(first, first + TILE)
                three(bank(X, f"{kind}{c}{h}", i)[:, :], [(lh, ll, wah[:, cols], wal[:, cols])], f"{kind}{c}{h}", X)

            def queries(X, name, i):
                h, j = int(name[0]), int(name[1])
                b = bank(X, f"Q{name}", i)
                for n in range(2):
                    cols = slice((2 * j + n) * P, (2 * j + n + 1) * P)
                    three(b[:, n * 2 * P:(n + 1) * 2 * P], [(wah[:, cols], wal[:, cols], ahh[h][:, :], ahl[h][:, :])],
                          f"Q{name}" if n else None, X)

            def transposed_keys(X, c, i):
                for j in range(2):
                    pe.wait_ge(*X["dve"].done(f"phi_K{c}{j}", i))
                    transposes(bank(X, f"KT{c}{j}", i),
                               [kt_[c % 2][:, (4 * j + n) * P:(4 * j + n + 1) * P] for n in range(4)], X["pe"], f"KT{c}{j}")

            def scores(X, c, j, i):
                pe.wait_ge(*X["act"].done(f"kf{c}{j}", i))
                if c % 2 == 0:
                    pe.wait_ge(*X["dve"].done(f"phi_Q{c // 2}{2 * j + 1}", i))
                own = slice((c % 2) * P, (c % 2 + 1) * P)
                ba, bb = bank(X, f"S{c}a{j}", i), bank(X, f"S{c}b{j}", i)
                for n in range(4):
                    p, cols = 4 * j + n, slice(n * P, (n + 1) * P)
                    ia = nc.tensor.matmul(ba[:, cols], kf[0:DH, p, :], qf[c // 2][0:DH, p, own], start=True, stop=True)
                    ib = nc.tensor.matmul(bb[:, cols], kf[DH:P, p, :], qf[c // 2][DH:P, p, own], start=True, stop=True)
                ia.then_inc(*X["pe"].step(f"S{c}a{j}"))
                ib.then_inc(*X["pe"].step(f"S{c}b{j}"))

            all_before(pe, G)
            for h in range(2):
                norm(G, h, 0)
            pe.wait_ge(*G["dve"].done("hl1", 0))
            for j in range(4):
                queries(G, f"0{j}", 0)
            for kind in ("K", "V"):
                for h in range(2):
                    token_major(G, kind, 0, h, 0)
            transposed_keys(G, 0, 0)
            scores(G, 0, 0, 0)
            scores(G, 0, 1, 0)
            all_before(pe, L)

            with pe.Fori(0, NT) as i:
                for c in C:
                    k, n = c % 2, (c + 1) % Q
                    if n == 0:
                        pe.wait_ge(*L["dve"].done("hl0", i))
                    for h in range(2):
                        token_major(L, "K", n, h, i)
                        if c == 0:
                            token_major(L, "V", n, h, i)
                    if c:
                        pe.wait_ge(*L["dve"].done(f"am{c}b1", i))
                    else:
                        pe.wait_ge(*L["dve"].done("am0b1", i, 1))
                        pe.wait_ge(*L["dve"].done("phi_K11", i))
                    own = slice(k * P, (k + 1) * P)
                    for g, (p0, p1) in enumerate(OG):
                        b = bank(L, f"O{c}{g}", i)
                        for p in range(p0, p1):
                            o = (p - p0) * PW
                            nc.tensor.matmul(b[:, o:o + PW], qf[c // 2][:, p, own], state[:, p, :], start=True, stop=False)
                            for m in range(2):
                                ins = nc.tensor.matmul(b[:, o + m * HW:o + (m + 1) * HW], am[:, 2 * (p // 4) + m, p % 4, :],
                                                       vt[k][:, 2 * p + m, :], start=False, stop=(m == 1))
                        ins.then_inc(*L["pe"].step(f"O{c}{g}"))
                        if g < len(QJOBS[c]):
                            if g == 0 and c % 2 == 0:
                                pe.wait_ge(*L["dve"].done("hl1" if c == 0 else "hl0", i, 1 if c == 0 else 0))
                            queries(L, QJOBS[c][g], i)
                            if c:
                                token_major(L, "V", n, g, i)
                    transposed_keys(L, n, i)
                    for g, (p0, p1) in enumerate(OG):
                        b = bank(L, f"D{c}{g}", i)
                        for p in range(p0, p1):
                            o = (p - p0) * PW
                            ins = nc.tensor.matmul(b[:, o:o + PW], kt_[k][:, p * P:(p + 1) * P],
                                                   vt[k][:, 2 * p:2 * p + 2, :], start=True, stop=True)
                        ins.then_inc(*L["pe"].step(f"D{c}{g}"))
                        if c % 2 and g == 1:
                            norm(L, c // 2, i)
                    pe.wait_ge(*L["dve"].done(f"on{c}2", i))
                    for j in range(2):
                        transposes(bank(L, f"OT{c}{j}", i), [ot[:, 2 * p:2 * p + 2, :] for p in range(4 * j, 4 * j + 4)],
                                   L["pe"], f"OT{c}{j}")
                    scores(L, n, 0, i)
                    if c % 2:
                        pe.wait_ge(*L["dve"].done(f"ol{c}1", i))
                        three(bank(L, f"WO{c // 2}", i)[:, 0:2 * P],
                              [(wah[:, 3 * DA + p * P:3 * DA + (p + 1) * P], wal[:, 3 * DA + p * P:3 * DA + (p + 1) * P],
                                oh[:, p, :], ol[:, p, :]) for p in range(PR)], f"WO{c // 2}", L)
                    scores(L, n, 1, i)
                pe.wait_ge(*L["act"].done("wf1", i))
                transposes(bank(L, "yT", i), [ayf[:, q * P:(q + 1) * P] for q in range(Q)], L["pe"], "yT")

            ffn_pe(ffn2)
            ffn_pe(ffn3)

        @block.scalar
        def _(act):
            def ffn_act(f):
                G, L = f["pro"], f["loop"]
                tern = f["kind"] == "ternary"

                def normalised(dst, src):
                    if f["gain"]:
                        return nc.scalar.activation(dst, src, ACT.Identity, scale=f["gain"][0], bias=f["gain"][1])
                    return nc.scalar.copy(dst, src)

                all_before(act, G)
                for u, U in enumerate(PAIR):
                    act.wait_ge(*G["pe"].done(f"nT{U}", 0))
                    normalised(full[u][:, :], ps[u][:, :]).then_inc(*G["act"].step(f"hf{U}"))
                    normalised(nh[u][:, :], ps[u][:, :]).then_inc(*G["act"].step(f"hi_n{U}"))
                if f["n"] == 0:
                    W = weights
                    for k, (a, b) in enumerate(PIECES):
                        act.wait_ge(*W["pool" if k in LO_BY_POOL else "dve"].done(f"lo{k}", 0))
                        if k:
                            act.wait_ge(*W["act"].done(f"sum{k - 1}", 0))
                        nc.scalar.activation(junk[:, 0:b - a], wl[:, a:b].bitcast(F32), ACT.Abs,
                                             accum_out=rest_sum[:, k:k + 1]).then_inc(*W["act"].step(f"sum{k}"))
                all_before(act, L)

                def norm(u, U, i):
                    act.wait_ge(*L["pe"].done(f"nT{U}", i))
                    slot_free(act, f, f"n{U}", i)
                    src = ps[f["banks"].bank[f"nT{U}"]][:, :]
                    normalised(slot(f, f"n{U}")[:, :], src).then_inc(*L["act"].step(f"hf{U}"))
                    normalised(nh[u][:, :], src).then_inc(*L["act"].step(f"hi_n{U}"))

                def silu(U, i):
                    for m in range(KT):
                        k = f["gates"].index(f"{U}{m}")
                        act.wait_ge(*L["pe"].done(f"g{U}{m}", i))
                        if k >= NS:
                            act.wait_ge(*L["dve"].done("mul" + f["gates"][k - NS], i))
                        else:
                            last = max(j for j in range(len(f["gates"])) if j % NS == k)
                            act.wait_ge(*L["dve"].done("mul" + f["gates"][last], i, 1))
                        nc.scalar.activation(gate[k % NS][:, :], ps[f["banks"].bank[f"g{U}{m}"]][:, :], ACT.Silu,
                                             scale=sc[:, m:m + 1]).then_inc(*L["act"].step(f"silu{U}{m}"))

                def gelu(name, scale, u, U, i):
                    if name == "L1":
                        act.wait_ge(*L["pe"].done(f"W3{U}", i, 1))
                    for m in range(KT):
                        act.wait_ge(*L["pe"].done(f"{name}{U}{m}", i))
                        slot_free(act, f, f"{name}{U}{m}", i)
                        s_ = sc[:, scale + m:scale + m + 1] if scale is not None else 1.0
                        src = ps[f["banks"].bank[f"{name}{U}{m}"]][:, :]
                        nc.scalar.activation(slot(f, f"{name}{U}{m}")[:, :], src, ACT.Gelu, scale=s_)\
                            .then_inc(*L["act"].step(f"gelu_{name}{U}{m}"))
                        if hi_by(f["kind"], f"{name}{U}{m}") == "act":
                            nc.scalar.activation(ah[u][0][:, m, :], src, ACT.Gelu, scale=s_)\
                                .then_inc(*L["act"].step(f"hi_{name}{U}{m}"))

                def evacuate(u, U, i):
                    act.wait_ge(*L["pe"].done(f"W3{U}", i))
                    act.wait_ge(*L["pe"].done(f"yT{U}", i, 1))
                    nc.scalar.activation(yf[u][:, :], ps[f["banks"].bank[f"W3{U}"]][:, :], ACT.Identity,
                                         scale=s3[:, 0:1] if tern else 1.0).then_inc(*L["act"].step(f"y{U}"))

                with act.Fori(0, NI) as i:
                    nc.scalar.activation(warm[:, 0:1], power[:, 0:1], ACT.Silu if tern else ACT.Gelu)
                    if tern:
                        silu("A", i)
                        silu("B", i)
                        nc.scalar.activation(warm[:, 1:2], power[:, 0:1], ACT.Gelu)
                        gelu("H1", 2 * KT, 0, "A", i)
                        gelu("H1", 2 * KT, 1, "B", i)
                        norm(0, "A", i)
                        gelu("H2", 3 * KT, 0, "A", i)
                        gelu("H2", 3 * KT, 1, "B", i)
                        evacuate(0, "A", i)
                        norm(1, "B", i)
                        evacuate(1, "B", i)
                    else:
                        gelu("L1", None, 0, "A", i)
                        gelu("L1", None, 1, "B", i)
                        evacuate(0, "A", i)
                        norm(0, "A", i)
                        evacuate(1, "B", i)
                        norm(1, "B", i)

            ffn_act(ffn1)

            G, L = attn["pro"], attn["loop"]

            def exp_relu(X, name, i):
                k, src = X["phis"].place[name], ps[X["banks"].bank[name]]
                if X["phis"].prior(name):
                    last, back = X["phis"].prior(name)
                    act.wait_ge(*X["dve"].done(f"phi_{last}", i, back))
                act.wait_ge(*X["pe"].done(name, i))
                nc.scalar.activation(ee[k][:, :], src[:, :], ACT.Exp).then_inc(*X["act"].step(f"e_{name}"))
                nc.scalar.activation(rr[k][:, :], src[:, :], ACT.Relu).then_inc(*X["act"].step(f"r_{name}"))

            def norm(X, h, i):
                act.wait_ge(*X["pe"].done(f"nT{h}", i))
                if X["loop"] or h:
                    act.wait_ge(*X["dve"].done(f"hl{1 - h}", i, 0 if h else 1))
                nc.scalar.activation(ahf[:, :], ps[X["banks"].bank[f"nT{h}"]][:, 0:2 * P], ACT.Identity,
                                     scale=affine[:, 0:1], bias=affine[:, 1:2]).then_inc(*X["act"].step(f"hf{h}"))

            def values(X, c, h, i):
                if X["loop"] and h == 0:
                    act.wait_ge(*X["pe"].done(f"D{(c - 2) % Q}2", i, 1 if c in (1,) else 0))
                act.wait_ge(*X["pe"].done(f"V{c}{h}", i))
                nc.scalar.copy(vt[c % 2][:, h * H // 2:(h + 1) * H // 2, 0:DH],
                               ps[X["banks"].bank[f"V{c}{h}"]][:, :].rearrange("p (h d) -> p h d", d=DH))\
                    .then_inc(*X["act"].step(f"v{c}{h}"))

            def transposed_keys(X, c, i):
                for j in range(2):
                    act.wait_ge(*X["pe"].done(f"KT{c}{j}", i))
                    nc.scalar.copy(kf[:, 4 * j:4 * j + 4, :],
                                   ps[X["banks"].bank[f"KT{c}{j}"]][:, :].rearrange("p (k n) -> p k n", n=P))\
                        .then_inc(*X["act"].step(f"kf{c}{j}"))

            all_before(act, G)
            for h in range(2):
                norm(G, h, 0)
            for j in range(4):
                exp_relu(G, f"Q0{j}", 0)
            for h in range(2):
                exp_relu(G, f"K0{h}", 0)
            for h in range(2):
                values(G, 0, h, 0)
            transposed_keys(G, 0, 0)
            all_before(act, L)

            with act.Fori(0, NT) as i:
                for c in C:
                    n = (c + 1) % Q
                    for h in range(2):
                        exp_relu(L, f"K{n}{h}", i)
                        if c == 0:
                            values(L, n, h, i)
                    if c == 0:
                        act.wait_ge(*L["dve"].done("y", i, 1))
                        nc.scalar.copy(axc[:, :, :], axp[:, :, :]).then_inc(*L["act"].step("cp"))
                    for g, name in enumerate(QJOBS[c]):
                        exp_relu(L, f"Q{name}", i)
                        if c:
                            values(L, n, g, i)
                    transposed_keys(L, n, i)
                    if c % 2:
                        norm(L, c // 2, i)
                    for j in range(2):
                        act.wait_ge(*L["pe"].done(f"OT{c}{j}", i))
                        if j == 0 and c % 2 == 0:
                            act.wait_ge(*L["pe"].done(f"WO{1 - c // 2}", i, 0 if c else 1))
                        nc.scalar.copy(oh[:, 4 * j:4 * j + 4, (c % 2) * P:(c % 2 + 1) * P],
                                       ps[L["banks"].bank[f"OT{c}{j}"]][:, :].rearrange("p (k n) -> p k n", n=P))\
                            .then_inc(*L["act"].step(f"oh{c}{j}"))
                    if c % 2:
                        h = c // 2
                        act.wait_ge(*L["pe"].done(f"WO{h}", i))
                        if h == 0:
                            act.wait_ge(*L["pe"].done("yT", i, 1))
                        nc.scalar.copy(ayf[:, h * 2 * P:(h + 1) * 2 * P], ps[L["banks"].bank[f"WO{h}"]][:, 0:2 * P])\
                            .then_inc(*L["act"].step(f"wf{h}"))

            ffn_act(ffn2)
            ffn_act(ffn3)

        @block.vector
        def _(dve):
            S = setup["dve"]
            nc.vector.memset(power[:, 0:1], -0.5).then_inc(pe_did, PRIME)
            nc.vector.memset(power[:, 1:2], -0.5).then_inc(act_did, PRIME)
            nc.vector.memset(power[:, 2:3], -0.5).then_inc(pool_did, PRIME)
            nc.vector.memset(power[:, 3:4], -0.5).then_inc(dve_did, PRIME)
            for k, s_ in enumerate((*out_x, out_y, out_xs)):
                nc.vector.memset(spare[:, k + 1:k + 2], 0.0).then_inc(s_, 16)
            nc.vector.memset(s3[:, :], 0.0).then_inc(*S.step("prime"))
            dve.wait_ge(*S.done("prime", 0))
            dve.wait_ge(in_v, 16)
            nc.vector.tensor_scalar(s3[:, :], sc[:, 4 * KT:4 * KT + 1], 0.5, None, ALU.mult).then_inc(*S.step("s3"))

            def ffn_dve(f):
                G, L, n, kind = f["pro"], f["loop"], f["n"], f["kind"]
                tern = kind == "ternary"

                def stats(u, U, X, i, arrived):
                    dve.wait_ge(in_ln[u], arrived)
                    for q in range(Q):
                        ins = nc.vector.bn_stats(bst[u][:, q, :], xln[u][:, q, :])
                    ins.then_inc(*X["dve"].step(f"st{U}"))
                    dve.wait_ge(*X["dve"].done(f"st{U}", i))
                    nc.vector.memset(spare[:, 0:1], 0.0)
                    for q in range(Q):
                        ins = nc.vector.bn_aggr(bag[u][:, q, :], bst[u][:, q, :])
                    ins.then_inc(*X["dve"].step(f"ag{U}"))
                    dve.wait_ge(*X["dve"].done(f"ag{U}", i))
                    nc.vector.tensor_scalar(ve[u][:, :], bag[u][:, :, 1], EPS_LN, None, ALU.add)\
                        .then_inc(*X["dve"].step(f"ve{U}"))

                def normalise(u, U, X, i):
                    dve.wait_ge(*X["pool"].done(f"rs{U}", i))
                    if X is L:
                        dve.wait_ge(*X["pe"].done(f"nT{U}", i, 1))
                    for q in range(Q):
                        ins = nc.vector.tensor_scalar(xn[u][:, q, :], xln[u][:, q, :], bag[u][:, q, 0:1],
                                                      rs[u][:, q:q + 1], ALU.subtract, ALU.mult)
                    ins.then_inc(*X["dve"].step(f"xn{U}"))

                if n < 2:
                    for u, U in enumerate(PAIR):
                        stats(u, U, G, 0, 16 * (f["loads"] + 1))
                    for u, U in enumerate(PAIR):
                        normalise(u, U, G, 0)
                all_before(dve, G)
                if n == 0:
                    S = weights["dve"]
                    for k, (a, b) in enumerate(PIECES):
                        dve.wait_ge(in_w[k], 16)
                        nc.vector.tensor_copy(wh[:, a:b], wst[:, a:b]).then_inc(*S.step(f"hi{k}"))
                        if k not in LO_BY_POOL:
                            dve.wait_ge(*S.done(f"hi{k}", 0))
                            nc.vector.tensor_tensor(wl[:, a:b], wst[:, a:b], wh[:, a:b].bitcast(F32), ALU.subtract)\
                                .then_inc(*S.step(f"lo{k}"))
                    dve.wait_ge(in_f, 16)
                    nc.vector.tensor_copy(fh[:, :], sf[:, :]).then_inc(*S.step("fhi"))
                    dve.wait_ge(*S.done("fhi", 0))
                    nc.vector.tensor_tensor(fl[:, :], sf[:, :], fh[:, :].bitcast(F32), ALU.subtract).then_inc(*S.step("flo"))
                    dve.wait_ge(*weights["pe"].done("flag", 0))
                    nc.vector.reduce_sum(flag[:, :], ps[7][0:1, 0:NPC], mybir.AxisListType.X).then_inc(*S.step("flag"))
                all_before(dve, L)

                def split(name, dst, m, u, U, i):
                    src, hi, lo = slot(f, name), ah[u][dst][:, m, :], al[u][dst][:, m, :]
                    if hi_by(kind, name) == "dve":
                        nc.vector.tensor_copy(hi, src[:, :]).then_inc(*L["dve"].step(f"hi_{name}"))
                    if lo_by(kind, name) == "dve":
                        dve.wait_ge(*L[hi_by(kind, name)].done(f"hi_{name}", i))
                        nc.vector.tensor_tensor(lo, src[:, :], hi.bitcast(F32), ALU.subtract)\
                            .then_inc(*L["dve"].step(f"lo_{name}"))

                def gated(u, U, i):
                    dve.wait_ge(*L["pe"].done(f"W3{U}", i, 1))
                    for m in range(KT):
                        name = f"{U}{m}"
                        k = f["gates"].index(name)
                        dve.wait_ge(*L["pe"].done(f"v{name}", i))
                        dve.wait_ge(*L["act"].done(f"silu{name}", i))
                        slot_free(dve, f, f"L1{name}", i)
                        nc.vector.scalar_tensor_tensor(slot(f, f"L1{name}")[:, :], ps[f["banks"].bank[f"v{name}"]][:, :],
                                                       sc[:, KT + m:KT + m + 1], gate[k % NS][:, :], ALU.mult, ALU.mult)\
                            .then_inc(*L["dve"].step(f"mul{name}"))
                        dve.wait_ge(*L["dve"].done(f"mul{name}", i))
                        split(f"L1{name}", 0, m, u, U, i)

                def activated(name, dst, reader, back, m, u, U, i):
                    if m == 0:
                        dve.wait_ge(*L["pe"].done(reader, i, back))
                    dve.wait_ge(*L["act"].done(f"gelu_{name}{U}{m}", i))
                    split(f"{name}{U}{m}", dst, m, u, U, i)

                with dve.Fori(0, NI) as i:
                    arrived = i * 16 + 16 * (f["loads"] + (2 if n < 2 else 0))
                    if tern:
                        gated(0, "A", i)
                        gated(1, "B", i)
                        for u, U in enumerate(PAIR):
                            for m in range(KT):
                                activated("H1", 1, f"H2{U}{KT - 1}", 1, m, u, U, i)
                                if m == 1:
                                    stats(u, U, L, i, arrived)
                            normalise(u, U, L, i)
                        for u, U in enumerate(PAIR):
                            for m in range(KT):
                                activated("H2", 0, f"H1{U}{KT - 1}", 0, m, u, U, i)
                                if n == 0 and u == 0 and m in (1, 2):
                                    cols = bass.ds(i * DA, DA)
                                    if m == 1:
                                        dve.wait_ge(in_a, i * 16 + 16)
                                        nc.vector.tensor_copy(wah[:, cols], stage[:, :]).then_inc(*L["dve"].step("ahi"))
                                    else:
                                        dve.wait_ge(*L["dve"].done("ahi", i))
                                        nc.vector.tensor_tensor(wal[:, cols], stage[:, :], wah[:, cols].bitcast(F32),
                                                                ALU.subtract).then_inc(*L["dve"].step("alo"))
                    else:
                        for u, U in enumerate(PAIR):
                            if u == 0:
                                stats(u, U, L, i, arrived)
                            for m in range(KT):
                                activated("L1", 0, f"W3{U}", 1, m, u, U, i)
                            if u == 1:
                                stats(u, U, L, i, arrived)
                            normalise(u, U, L, i)
                    for u, U in enumerate(PAIR):
                        dve.wait_ge(*L["pe"].done(f"yT{U}", i))
                        dve.wait_ge(in_res[u], i * 16 + 16 * (n * NI + 1))
                        dve.wait_ge(out_x[u], i * 16 + 16 * (n * NI + 1))
                        nc.vector.tensor_tensor(xo[u][:, :, :], ps[f["banks"].bank[f"yT{U}"]][:, :].rearrange("p (q d) -> p q d", d=D),
                                                xres[u][:, :, :], ALU.add).then_inc(*L["dve"].step(f"res{U}"))

            ffn_dve(ffn1)

            G, L = attn["pro"], attn["loop"]

            def small(X, name, i, ins):
                ins.then_inc(*X["dve"].step(name))
                dve.wait_ge(*X["dve"].done(name, i))

            def phi(X, name, i):
                if name[0] == "Q":
                    h, j = int(name[1]), int(name[2])
                    dst = qf[h][:, 2 * j:2 * j + 2, :]
                    if X["loop"] and j == 0:
                        dve.wait_ge(*X["pe"].done(f"O{2 * h + 1}2", i, h))
                else:
                    c, h = int(name[1]), int(name[2])
                    dst = kt_[c % 2][:, h * TILE:(h + 1) * TILE]
                    if X["loop"] and h == 0:
                        dve.wait_ge(*X["pe"].done(f"D{(c - 2) % Q}2", i, 1 if c == 1 else 0))
                k = X["phis"].place[name]
                dve.wait_ge(*X["act"].done(f"r_{name}", i))
                nc.vector.scalar_tensor_tensor(dst, ee[k][:, :], 1.0, rr[k][:, :], ALU.min, ALU.add)\
                    .then_inc(*X["dve"].step(f"phi_{name}"))

            def stats(X, i):
                dve.wait_ge(in_ax, i * 16 + (32 if X["loop"] else 16))
                for q in range(Q):
                    ins = nc.vector.bn_stats(abst[:, q, :], ax[:, q, :])
                small(X, "st", i, ins)
                nc.vector.memset(spare[:, 0:1], 0.0)
                for q in range(Q):
                    ins = nc.vector.bn_aggr(abag[:, q, :], abst[:, q, :])
                small(X, "ag", i, ins)
                nc.vector.tensor_scalar(av[:, :], abag[:, :, 1], EPS_LN, None, ALU.add).then_inc(*X["dve"].step("ve"))

            def once(X, i):
                dve.wait_ge(*X["pool"].done("r1", i))
                small(X, "v1", i, nc.vector.tensor_tensor(av1[:, :], abag[:, :, 1], ar1[:, :], ALU.mult))
                small(X, "v2", i, nc.vector.tensor_tensor(av2[:, :], av1[:, :], ar1[:, :], ALU.mult))
                nc.vector.tensor_scalar(av3[:, :], av2[:, :], EPS_LN, None, ALU.add).then_inc(*X["dve"].step("v3"))
                if X["loop"]:
                    dve.wait_ge(*X["act"].done("cp", i))
                for q in range(Q):
                    ins = nc.vector.tensor_scalar(axp[:, q, :], ax[:, q, :], abag[:, q, 0:1], ar1[:, q:q + 1],
                                                  ALU.subtract, ALU.mult)
                ins.then_inc(*X["dve"].step("xp"))

            def twice(X, i):
                dve.wait_ge(*X["pool"].done("r2", i))
                dve.wait_ge(*X["dve"].done("xp", i))
                if X["loop"]:
                    dve.wait_ge(*X["pe"].done("nT1", i, 1))
                for q in range(Q):
                    ins = nc.vector.tensor_scalar(axn[:, q, :], axp[:, q, :], ar2[:, q:q + 1], None, ALU.mult)
                ins.then_inc(*X["dve"].step("xn"))

            def norm(X, h, i):
                dve.wait_ge(*X["act"].done(f"hf{h}", i))
                if X["loop"]:
                    dve.wait_ge(*X["pe"].done(("Q13", "V31")[h] if h else "V11", i, 0))
                nc.vector.tensor_copy(ahh[h][:, :], ahf[:, :]).then_inc(*X["dve"].step(f"hh{h}"))
                dve.wait_ge(*X["dve"].done(f"hh{h}", i))
                nc.vector.tensor_tensor(ahl[h][:, :], ahf[:, :], ahh[h][:, :].bitcast(F32), ALU.subtract)\
                    .then_inc(*X["dve"].step(f"hl{h}"))

            def masked(X, c, j, i):
                for g in ("a", "b"):
                    dve.wait_ge(*X["pe"].done(f"S{c}{g}{j}", i))
                    nc.vector.tensor_tensor(am[:, 2 * j + (g == "b"), :, :],
                                            ps[X["banks"].bank[f"S{c}{g}{j}"]][:, :].rearrange("p (h n) -> p h n", n=P),
                                            mask[:, :, :], ALU.mult).then_inc(*X["dve"].step(f"am{c}{g}{j}"))

            stats(G, 0)
            all_before(dve, G)
            for k in range(2):
                nc.vector.memset(vt[k][:, :, DH:DH + 1], 1.0)
                nc.vector.memset(vt[k][:, :, DH + 1:DH + 2], 0.0)
            once(G, 0)
            twice(G, 0)
            for h in range(2):
                norm(G, h, 0)
            for j in range(4):
                phi(G, f"Q0{j}", 0)
            for h in range(2):
                phi(G, f"K0{h}", 0)
            masked(G, 0, 0, 0)
            masked(G, 0, 1, 0)
            all_before(dve, L)

            with dve.Fori(0, NB) as b_:
                nc.vector.memset(state[:, :, :], 0.0)
                with dve.Fori(0, SUP) as s_:
                    i = b_ * SUP + s_
                    for c in C:
                        n = (c + 1) % Q
                        for h in range(2):
                            phi(L, f"K{n}{h}", i)
                        dve.wait_ge(*L["pe"].done(f"OT{(c - 1) % Q}1", i, 0 if c else 1))
                        for g, (p0, p1) in enumerate(OG):
                            nh_ = 2 * (p1 - p0)
                            src = ps[L["banks"].bank[f"O{c}{g}"]][:, 0:nh_ * HW].rearrange("p (h w) -> p h w", w=HW)
                            dve.wait_ge(*L["pe"].done(f"O{c}{g}", i))
                            small(L, f"dm{c}{g}", i, nc.vector.tensor_scalar(den[:, g, 0:nh_], src[:, :, DH], EPS_DEN, None, ALU.max))
                            small(L, f"rd{c}{g}", i, nc.vector.reciprocal(rden[:, g, 0:nh_], den[:, g, 0:nh_]))
                            nc.vector.tensor_tensor(ot[:, 2 * p0:2 * p1, :], src[:, :, 0:DH],
                                                    rden[:, g, 0:nh_].unsqueeze(2).to_broadcast([P, nh_, DH]), ALU.mult)\
                                .then_inc(*L["dve"].step(f"on{c}{g}"))
                            if g < len(QJOBS[c]):
                                phi(L, f"Q{QJOBS[c][g]}", i)
                            if c == 1 and g == 0:
                                once(L, i)
                        if c == 1:
                            twice(L, i)
                        for g, (p0, p1) in enumerate(OG):
                            src = ps[L["banks"].bank[f"D{c}{g}"]][:, 0:(p1 - p0) * PW].rearrange("p (k w) -> p k w", w=PW)
                            dve.wait_ge(*L["pe"].done(f"D{c}{g}", i))
                            for name, rows, cols in (("sa", slice(0, DH), slice(0, HW)), ("sb", slice(DH, P), slice(HW, PW))):
                                nc.vector.tensor_tensor(state[rows, p0:p1, cols], src[rows, :, cols], state[rows, p0:p1, cols],
                                                        ALU.add).then_inc(*L["dve"].step(f"{name}{c}{g}"))
                        if c == 0:
                            stats(L, i)
                        for j in range(2):
                            dve.wait_ge(*L["act"].done(f"oh{c}{j}", i))
                            own = slice((c % 2) * P, (c % 2 + 1) * P)
                            nc.vector.tensor_tensor(ol[:, 4 * j:4 * j + 4, own],
                                                    ps[L["banks"].bank[f"OT{c}{j}"]][:, :].rearrange("p (k n) -> p k n", n=P),
                                                    oh[:, 4 * j:4 * j + 4, own].bitcast(F32), ALU.subtract)\
                                .then_inc(*L["dve"].step(f"ol{c}{j}"))
                        masked(L, n, 0, i)
                        masked(L, n, 1, i)
                        if c % 2:
                            norm(L, c // 2, i)
                    dve.wait_ge(*L["pe"].done("yT", i))
                    dve.wait_ge(out_y, i * 16 + 16)
                    dve.wait_ge(*L["pool"].done("ys", i, 1))
                    nc.vector.tensor_tensor(ay[:, :, :], ps[L["banks"].bank["yT"]][:, :].rearrange("p (q d) -> p q d", d=D),
                                            axc[:, :, :], ALU.add).then_inc(*L["dve"].step("y"))

            ffn_dve(ffn2)
            ffn_dve(ffn3)

        @block.gpsimd
        def _(pool):
            S = setup["pool"]
            pool.wait_ge(pool_did, PRIME)
            nc.gpsimd.memset(ident[:, :], 0.0).then_inc(*S.step("id0"))
            pool.wait_ge(*S.done("id0", 0))
            nc.gpsimd.affine_select(out=ident[:, :], in_=ident[:, :], compare_op=ALU.not_equal, fill=1.0, base=0,
                                    pattern=[[-1, P]], channel_multiplier=1).then_inc(*S.step("ident"))
            nc.gpsimd.memset(ones[:, :], 1.0).then_inc(*S.step("ones"))
            nc.gpsimd.memset(mask[:, :, :], 1.0).then_inc(*S.step("mask1"))
            pool.wait_ge(*S.done("mask1", 0))
            nc.gpsimd.affine_select(out=mask[:, :, :], in_=mask[:, :, :], compare_op=ALU.is_ge, fill=0.0, base=0,
                                    pattern=[[0, 4], [1, P]], channel_multiplier=-1).then_inc(*S.step("mask"))

            def ffn_pool(f):
                G, L = f["pro"], f["loop"]
                tern = f["kind"] == "ternary"

                def rest(X, name, src, hi, dst, i):
                    if lo_by(f["kind"], name) == "pool":
                        pool.wait_ge(*X[hi_by(f["kind"], name)].done(f"hi_{name}", i))
                        nc.gpsimd.tensor_tensor(dst, src[:, :], hi.bitcast(F32), ALU.subtract)\
                            .then_inc(*X["pool"].step(f"lo_{name}"))

                def rstd(u, U, X, i):
                    pool.wait_ge(*X["dve"].done(f"ve{U}", i))
                    nc.gpsimd.tensor_tensor(rs[u][:, :], ve[u][:, :], power[:, :], ALU.pow).then_inc(*X["pool"].step(f"rs{U}"))

                if f["n"] < 2:
                    for u, U in enumerate(PAIR):
                        rstd(u, U, G, 0)
                all_before(pool, G)
                for u, U in enumerate(PAIR):
                    rest(G, f"n{U}", full[u], nh[u][:, :], nl[u][:, :], 0)
                if f["n"] == 0:
                    for k in LO_BY_POOL:
                        a, b = PIECES[k]
                        pool.wait_ge(*weights["dve"].done(f"hi{k}", 0))
                        nc.gpsimd.tensor_tensor(wl[:, a:b], wst[:, a:b], wh[:, a:b].bitcast(F32), ALU.subtract)\
                            .then_inc(*weights["pool"].step(f"lo{k}"))
                all_before(pool, L)

                def low(name, dst, m, u, U, i):
                    rest(L, f"{name}{U}{m}", slot(f, f"{name}{U}{m}"), ah[u][dst][:, m, :], al[u][dst][:, m, :], i)

                def norm(u, U, i):
                    rest(L, f"n{U}", slot(f, f"n{U}"), nh[u][:, :], nl[u][:, :], i)

                with pool.Fori(0, NI) as i:
                    if tern:
                        for u, U in enumerate(PAIR):
                            for m in range(KT):
                                low("L1", 0, m, u, U, i)
                        for u, U in enumerate(PAIR):
                            for m in range(KT):
                                low("H1", 1, m, u, U, i)
                                if m == 2:
                                    rstd(u, U, L, i)
                        norm(0, "A", i)
                        for u, U in enumerate(PAIR):
                            for m in range(KT):
                                low("H2", 0, m, u, U, i)
                        norm(1, "B", i)
                    else:
                        for u, U in enumerate(PAIR):
                            for m in range(KT):
                                low("L1", 0, m, u, U, i)
                                if m == (0, KT - 1)[u]:
                                    rstd(u, U, L, i)
                        for u, U in enumerate(PAIR):
                            norm(u, U, i)

            ffn_pool(ffn1)

            G, L = attn["pro"], attn["loop"]

            def root(X, name, after, dst, src, i):
                pool.wait_ge(*X["dve"].done(after, i))
                nc.gpsimd.tensor_tensor(dst[:, :], src[:, :], power[:, :], ALU.pow).then_inc(*X["pool"].step(name))

            root(G, "r1", "ve", ar1, av, 0)
            all_before(pool, G)
            root(G, "r2", "v3", ar2, av3, 0)
            all_before(pool, L)
            with pool.Fori(0, NT) as i:
                root(L, "r1", "ve", ar1, av, i)
                root(L, "r2", "v3", ar2, av3, i)
                pool.wait_ge(*L["dve"].done("y", i))
                pool.wait_ge(in_ar, i * 16 + 16)
                pool.wait_ge(out_xs, i * 16 + 16)
                nc.gpsimd.tensor_tensor(axs[:, :, :], ay[:, :, :], axr[:, :, :], ALU.add).then_inc(*L["pool"].step("ys"))

            ffn_pool(ffn2)
            ffn_pool(ffn3)


def kernel(**inputs):
    import numpy as np
    import concourse.bacc as bacc
    from concourse.bass_utils import run_bass_kernel_spmd

    nc = bacc.Bacc("TRN2", target_bir_lowering=False, num_devices=1)
    w = {name: np.asarray(a) for name, a in inputs.items()}
    x = w["L0_attn_x"]

    def by_partition(a):
        return a.reshape(-1, P, a.shape[1]).transpose(1, 0, 2).reshape(P, -1)

    arrays = {
        "L0_attn_x": x,
        "ternary": np.concatenate([by_partition(w[f"L0_ffn_{n}_w"].T) for n in ("w1", "w2", "h1", "h2", "w3")], axis=1),
        "plain": np.concatenate([by_partition(w["L0_attn_Wf1"]), by_partition(w["L0_attn_Wf2"])], axis=1),
        "attn": np.stack([by_partition(w[f"L0_attn_{n}"]) for n in ("Wq", "Wk", "Wv", "Wo")]),
        "vectors": np.concatenate([w[f"L0_ffn_{n}_s"].reshape(-1, P).T for n in ("w1", "w2", "h1", "h2", "w3")]
                                  + [w[f"L0_attn_{n}"].reshape(-1, P).T for n in ("ln1_g", "ln1_b", "ln2_g", "ln2_b")], axis=1),
    }
    arrays = {f"in_{name}": np.ascontiguousarray(a) for name, a in arrays.items()}
    args = {name[3:]: nc.dram_tensor(name, a.shape, mybir.dt.from_np(a.dtype), kind="ExternalInput").ap()
            for name, a in arrays.items()}
    out = nc.dram_tensor("out_0", x.shape, mybir.dt.from_np(x.dtype), kind="ExternalOutput").ap()
    build_kernel(nc, args, out.rearrange("b t d -> (b t) d"))
    got = run_bass_kernel_spmd(nc, [arrays], core_ids=[0])
    return got.results[0]["out_0"]
```
